# Optimizing a Trainium2 kernel written in Bass

```python
import numpy as np
import jax
import jax.numpy as jnp

def _softmax(x, axis=-1):
    return jax.nn.softmax(x, axis=axis)

def _gelu(x):
    return jax.nn.gelu(x, approximate=True)

def _silu(x):
    return jax.nn.silu(x)

def _sigmoid(x):
    return jax.nn.sigmoid(x)

def _layernorm(x, axis=-1, eps=1e-05):
    m = jnp.mean(x, axis=axis, keepdims=True)
    v = jnp.var(x, axis=axis, keepdims=True)
    return (x - m) / jnp.sqrt(v + eps)

def _scatter_add(tgt, idx, src, axis=0):
    return tgt.at[idx].add(src)

def _segment_sum(src, seg, n):
    return jax.ops.segment_sum(src, seg, n)
kernel_name = 'mk_adaln_attn_ffn_d1_seqx_r4_ad8853'

def setup_inputs(seed: int=0):
    np.random.seed(seed)
    _w = jnp.asarray

    def _rec_inputs():
        import jax
        import jax.numpy as jnp
        _rk = jax.random.key(seed)
        x = -7.109e-05 + 0.9999 * jax.random.normal(jax.random.fold_in(_rk, 1), (32, 64, 1024), jnp.float32)
        _lenS = 64 - jax.random.randint(jax.random.fold_in(_rk, 7), (32,), 0, max(1, 64 // 4) + 1, jnp.int32)
        _lenS2 = 64 - jax.random.randint(jax.random.fold_in(_rk, 8), (32,), 0, max(1, 64 // 4) + 1, jnp.int32)
        itok_B_0_15 = jax.random.randint(jax.random.fold_in(_rk, 11), (32,), 0, 16, jnp.int32)
        itok_B_6_15 = jax.random.randint(jax.random.fold_in(_rk, 12), (32,), 6, 16, jnp.int32)
        return (x, itok_B_0_15, itok_B_6_15)
    x, itok_B_0_15, itok_B_6_15 = _rec_inputs()

    def _L0_cond_setup():
        import jax, jax.numpy as jnp
        import numpy as np
        SCALING = 16.0 / 16
        key = jax.random.key(seed)
        k1, k2, k3, k4, k5 = jax.random.split(key, 5)
        B, S, D_IN, D_OUT, R, N_ADPT = (8, 512, 1024, 1024, 16, 16)
        x = jax.random.normal(k1, (B, S, D_IN), dtype=jnp.float32)
        adapter_indices = jax.random.randint(k2, (B,), 0, N_ADPT, dtype=jnp.int32)
        W = jax.random.normal(k3, (D_IN, D_OUT), dtype=jnp.float32) * 0.02
        lora_A = jax.random.normal(k4, (N_ADPT, D_IN, R), dtype=jnp.float32) * 0.02
        lora_B = jax.random.normal(k5, (N_ADPT, R, D_OUT), dtype=jnp.float32) * 0.02
        return {'x': x, 'adapter_indices': adapter_indices, 'W': W, 'lora_A': lora_A, 'lora_B': lora_B}
    _L0_cond_all = _L0_cond_setup()
    _L0_cond_in = {k: v for k, v in _L0_cond_all.items() if k in ('W', 'lora_A', 'lora_B')}
    del _L0_cond_all

    def _L0_attn_setup():
        import jax, jax.numpy as jnp
        import numpy as np
        import math
        D_MODEL = 512
        D_STATE = 16
        EXPAND = 2
        D_INNER = D_MODEL * EXPAND
        DT_RANK = math.ceil(D_MODEL / 16)
        BATCH, SEQ_LEN = (2, 128)
        key = jax.random.key(seed)
        ks = jax.random.split(key, 6)
        x = jax.random.normal(ks[0], (BATCH, SEQ_LEN, D_INNER), dtype=jnp.float32)
        A_log = jnp.log(jax.random.uniform(ks[1], (D_INNER, D_STATE), minval=0.5, maxval=16.0, dtype=jnp.float32))
        D = jnp.ones((D_INNER,), dtype=jnp.float32)
        x_proj_w = 0.02 * jax.random.normal(ks[2], (DT_RANK + 2 * D_STATE, D_INNER), dtype=jnp.float32)
        dt_init_std = DT_RANK ** (-0.5)
        dt_proj_w = jax.random.uniform(ks[3], (D_INNER, DT_RANK), minval=-dt_init_std, maxval=dt_init_std, dtype=jnp.float32)
        dt = jnp.exp(jax.random.uniform(ks[4], (D_INNER,), dtype=jnp.float32) * (math.log(0.1) - math.log(0.001)) + math.log(0.001))
        dt = jnp.clip(dt, 0.0001, None)
        dt_proj_b = dt + jnp.log(-jnp.expm1(-dt))
        return {'x': x, 'A_log': A_log, 'D': D, 'x_proj_w': x_proj_w, 'dt_proj_w': dt_proj_w, 'dt_proj_b': dt_proj_b}
    _L0_attn_all = _L0_attn_setup()
    _L0_attn_in = {k: v for k, v in _L0_attn_all.items() if k in ('A_log', 'D', 'x_proj_w', 'dt_proj_w', 'dt_proj_b')}
    del _L0_attn_all

    def _L0_cond2_setup():
        import jax, jax.numpy as jnp
        import numpy as np
        B, S, D_IN, D_OUT = (4, 512, 1024, 1024)
        RANK, MAX_LORAS = (16, 32)
        key = jax.random.key(seed)
        ks = jax.random.split(key, 6)
        x = jax.random.normal(ks[0], (B, S, D_IN), dtype=jnp.float32)
        adapter_ids = jax.random.randint(ks[1], (B,), 0, MAX_LORAS)
        base_weight = jax.random.normal(ks[2], (D_OUT, D_IN), dtype=jnp.float32) * D_IN ** (-0.5)
        base_bias = jax.random.normal(ks[3], (D_OUT,), dtype=jnp.float32) * 0.01
        lora_A_w = jax.random.normal(ks[4], (MAX_LORAS, RANK, D_IN), dtype=jnp.float32) * D_IN ** (-0.5)
        lora_B_w = jax.random.normal(ks[5], (MAX_LORAS, D_OUT, RANK), dtype=jnp.float32) * RANK ** (-0.5)
        return {'x': x, 'adapter_ids': adapter_ids, 'base_weight': base_weight, 'base_bias': base_bias, 'lora_A_w': lora_A_w, 'lora_B_w': lora_B_w}
    _L0_cond2_all = _L0_cond2_setup()
    _L0_cond2_in = {k: v for k, v in _L0_cond2_all.items() if k in ('base_weight', 'base_bias', 'lora_A_w', 'lora_B_w')}
    del _L0_cond2_all

    def _L0_ffn_setup():
        import jax, jax.numpy as jnp
        import numpy as np
        LORA_SCALE = 16.0 / jnp.sqrt(16.0)
        TOP_K = 2
        key = jax.random.key(seed)
        k1, k2, k3, k4 = jax.random.split(key, 4)
        B_, S, D, O, E, R = (4, 512, 1024, 1024, 4, 16)
        x = jax.random.normal(k1, (B_, S, D), dtype=jnp.float32)
        router_w = jax.random.normal(k2, (E, D), dtype=jnp.float32) * 0.02
        A = jax.random.normal(k3, (E, R, D), dtype=jnp.float32) * 0.02
        B = jax.random.normal(k4, (O,), dtype=jnp.float32)
        B = jax.random.normal(k4, (E, O, R), dtype=jnp.float32) * 0.02
        return {'x': x, 'router_w': router_w, 'A': A, 'B': B}
    _L0_ffn_all = _L0_ffn_setup()
    _L0_ffn_in = {k: v for k, v in _L0_ffn_all.items() if k in ('router_w', 'A', 'B')}
    del _L0_ffn_all
    return {'x': x, 'itok_B_0_15': itok_B_0_15, 'itok_B_6_15': itok_B_6_15, 'L0_cond_W': _L0_cond_in['W'], 'L0_cond_lora_A': _L0_cond_in['lora_A'], 'L0_cond_lora_B': _L0_cond_in['lora_B'], 'L0_attn_A_log': _L0_attn_in['A_log'], 'L0_attn_D': _L0_attn_in['D'], 'L0_attn_x_proj_w': _L0_attn_in['x_proj_w'], 'L0_attn_dt_proj_w': _L0_attn_in['dt_proj_w'], 'L0_attn_dt_proj_b': _L0_attn_in['dt_proj_b'], 'L0_cond2_base_weight': _L0_cond2_in['base_weight'], 'L0_cond2_base_bias': _L0_cond2_in['base_bias'], 'L0_cond2_lora_A_w': _L0_cond2_in['lora_A_w'], 'L0_cond2_lora_B_w': _L0_cond2_in['lora_B_w'], 'L0_ffn_router_w': _L0_ffn_in['router_w'], 'L0_ffn_A': _L0_ffn_in['A'], 'L0_ffn_B': _L0_ffn_in['B']}

def reference(x, itok_B_0_15, itok_B_6_15, L0_cond_W, L0_cond_lora_A, L0_cond_lora_B, L0_attn_A_log, L0_attn_D, L0_attn_x_proj_w, L0_attn_dt_proj_w, L0_attn_dt_proj_b, L0_cond2_base_weight, L0_cond2_base_bias, L0_cond2_lora_A_w, L0_cond2_lora_B_w, L0_ffn_router_w, L0_ffn_A, L0_ffn_B):
    import jax
    import jax.numpy as jnp

    def _L0_cond_ref(x, adapter_indices, W, lora_A, lora_B):
        import jax, jax.numpy as jnp
        import numpy as np
        SCALING = 16.0 / 16
        base_out = jnp.einsum('bsi,io->bso', x, W)
        A = lora_A[adapter_indices]
        Bm = lora_B[adapter_indices]
        xr = jnp.einsum('bsi,bir->bsr', x, A)
        lora_out = jnp.einsum('bsr,bro->bso', xr, Bm)
        return base_out + lora_out * SCALING

    def _L0_attn_ref(x, A_log, D, x_proj_w, dt_proj_w, dt_proj_b):
        import jax, jax.numpy as jnp
        import numpy as np
        import math
        D_MODEL = 512
        D_STATE = 16
        EXPAND = 2
        D_INNER = D_MODEL * EXPAND
        DT_RANK = math.ceil(D_MODEL / 16)
        BATCH, SEQ_LEN = (2, 128)
        A = -jnp.exp(A_log)
        xp = jnp.einsum('bld,rd->blr', x, x_proj_w)
        dt_in = xp[..., :DT_RANK]
        B = xp[..., DT_RANK:DT_RANK + D_STATE]
        C = xp[..., DT_RANK + D_STATE:]
        dt = jax.nn.softplus(jnp.einsum('blr,dr->bld', dt_in, dt_proj_w) + dt_proj_b)
        dA = jnp.exp(dt[..., None] * A)
        dBx = dt[..., None] * B[:, :, None, :] * x[..., None]

        def step(h, inp):
            dA_t, dBx_t, C_t = inp
            h = dA_t * h + dBx_t
            y = jnp.einsum('bdn,bn->bd', h, C_t)
            return (h, y)
        h0 = jnp.zeros((x.shape[0], D_INNER, D_STATE), dtype=x.dtype)
        _, ys = jax.lax.scan(step, h0, (jnp.moveaxis(dA, 1, 0), jnp.moveaxis(dBx, 1, 0), jnp.moveaxis(C, 1, 0)))
        y = jnp.moveaxis(ys, 0, 1) + D * x
        return y

    def _L0_cond2_ref(x, adapter_ids, base_weight, base_bias, lora_A_w, lora_B_w):
        import jax, jax.numpy as jnp
        import numpy as np
        B, S, D_IN, D_OUT = (4, 512, 1024, 1024)
        RANK, MAX_LORAS = (16, 32)
        result = jnp.einsum('bsd,od->bso', x, base_weight) + base_bias
        A = lora_A_w[adapter_ids]
        Bw = lora_B_w[adapter_ids]
        h = jnp.einsum('bsd,brd->bsr', x, A)
        lora_out = jnp.einsum('bsr,bor->bso', h, Bw)
        result = result + lora_out
        return result.astype(x.dtype)

    def _L0_ffn_ref(x, router_w, A, B):
        import jax, jax.numpy as jnp
        import numpy as np
        LORA_SCALE = 16.0 / jnp.sqrt(16.0)
        TOP_K = 2
        D = x.shape[-1]
        flat = x.reshape(-1, D)
        logits = flat @ router_w.T
        topk_vals, topk_idx = jax.lax.top_k(logits, TOP_K)
        sparse = jnp.full_like(logits, -jnp.inf)
        rows = jnp.arange(logits.shape[0])[:, None]
        sparse = sparse.at[rows, topk_idx].set(topk_vals)
        gates = jax.nn.softmax(sparse, axis=-1)
        mid = jnp.einsum('tf,erf->ter', flat, A)
        all_deltas = jnp.einsum('ter,eor->teo', mid, B) * LORA_SCALE
        delta = jnp.einsum('te,teo->to', gates, all_deltas)
        return delta.reshape(*x.shape[:-1], -1)
    x = x + _L0_attn_ref(_L0_cond_ref(x, itok_B_0_15, L0_cond_W, L0_cond_lora_A, L0_cond_lora_B), L0_attn_A_log, L0_attn_D, L0_attn_x_proj_w, L0_attn_dt_proj_w, L0_attn_dt_proj_b)
    x = x + _L0_ffn_ref(_L0_cond2_ref(x, itok_B_6_15, L0_cond2_base_weight, L0_cond2_base_bias, L0_cond2_lora_A_w, L0_cond2_lora_B_w), L0_ffn_router_w, L0_ffn_A, L0_ffn_B)
    return x

_drawn_inputs = setup_inputs


def setup_inputs(seed=0):
    import zlib

    import numpy as np

    out = dict(_drawn_inputs(seed))
    spreads = {'L0_attn_D': (1.0, 0.2)}
    factors = {'L0_attn_dt_proj_w': 3.035, 'L0_cond2_base_bias': 8.0}
    for name, (base, spread) in spreads.items():
        noise = np.random.default_rng([zlib.crc32(name.encode()), seed]).standard_normal(out[name].shape)
        drawn = base * np.exp(spread * noise) if base else spread * noise
        out[name] = jnp.asarray(drawn.astype(out[name].dtype))
    for name, factor in factors.items():
        out[name] = (out[name] * factor).astype(out[name].dtype)
    return out
```

```python
import concourse.bass as bass
from concourse import mybir
from contextlib import ExitStack

P = 128
BATCHES, STEPS, D = 32, 64, 1024
R = 16
GROUPS = 8
GB_ = BATCHES // GROUPS
T = GB_ * STEPS
TT = T // P
K = D // P
DTR = 32
E = 4
EM = E * R
HS = R // 2
UNIT = HS * P
UNITS = 4
QT = 32
NQ = T // QT
LAG = 3
NDA, NH, NHC, NDT = 2, 2, 4, 4
LORA2_SCALE = 16.0 / 16.0 ** 0.5

JOBS = {(j, u): [] for j in range(K) for u in range(UNITS)}
for _j in range(K):
    JOBS[_j, 1].append(("dtz", _j + 2))
    JOBS[_j, 2].append(("x1T", _j - 2))
    JOBS[_j, 3].append(("dtxT", _j + 2))
JOBS[0, 2] += [("xT", 0), ("xT", 1)]
JOBS[0, 3] += [("xT", 2), ("xT", 3)]
JOBS[1, 0] += [("xr", 0), ("cond", 0)]
JOBS[1, 2] += [("mid", 0), ("logit", 0)]
JOBS[1, 3] += [("midT", 0)]
JOBS[2, 0] += [("gm", 0), ("out", 0), ("out", 1)]
JOBS[2, 1] += [("out", 2), ("out", 3)]
for _o, _at in enumerate([(2, 3), (3, 0), (3, 2), (4, 0), (4, 2), (5, 0), (5, 3)]):
    JOBS[_at] += [("cond", _o + 1)]
JOBS[6, 0] += [("xproj", 0)]
JOBS[6, 2] += [("Bst", 0)]
JOBS[6, 3] += [("A2T", 0), ("A2T", 1)]
JOBS[7, 0] += [("FB", 0)]
BANK = {}
for _j in range(K):
    for _u in range(UNITS):
        for _job in JOBS[_j, _u]:
            BANK[_job] = len(BANK) % 2
assert len(BANK) % 2 == 0
OF_PREVIOUS = {"mid", "logit", "midT", "gm", "out"}
OF_NEXT = {"xT", "xr", "cond", "xproj", "Bst"}


def layer_kernel(nc, x, ids1, ids2, W, loraA, loraB, A_log, Dw, xproj_w, dtproj_w, dtproj_b,
                 W2, bias2, lora2A, lora2B, router_w, expA, expB, out):
    fp32, fr, i32 = mybir.dt.float32, mybir.dt.float32r, mybir.dt.int32
    ALU, ACT, AX = mybir.AluOpType, mybir.ActivationFunctionType, mybir.AxisListType
    DynSlice = bass.DynSlice

    ctx = ExitStack()
    with ctx:
        def sb(name, shape, dt=fp32):
            return ctx.enter_context(nc.sbuf_tensor(name, shape, dt))

        def sem(name):
            return ctx.enter_context(nc.semaphore(name))

        ident = sb("ident", [P, P])
        diag32 = sb("diag32", [P, QT])
        own_batch = sb("own_batch", [P, T])
        use_hi = sb("use_hi", [P, 1])
        use_lo = sb("use_lo", [P, 1])
        before = sb("before", [P, E, E])
        idx = sb("idx", [1, 2, BATCHES], i32)
        Wsb = sb("Wsb", [P, K, D])
        negA = sb("negA", [P, K, R])
        Dsb = sb("Dsb", [P, K])
        xprojT = sb("xprojT", [P, K, 2 * DTR])
        dtprojT = sb("dtprojT", [DTR + 1, D])
        FT = sb("FT", [P, K, EM + E])
        GA2T = sb("GA2T", [P, K, P])
        GTl = sb("GTl", [P, K, E])
        cmid = sb("cmid", [EM, 1])
        clog = sb("clog", [P, E])
        bias_sb = sb("bias_sb", [P, K])
        expBT = sb("expBT", [EM, D])

        xin = sb("xin", [P, 2, TT, 2 * P])
        xT = sb("xT", [P, K, T])
        GA = sb("GA", [P, K, GB_ * R])
        GBA2 = sb("GBA2", [P, D])
        B2g = sb("B2g", [P, K, GB_ * R])
        FB = sb("FB", [P, EM + E])
        low = sb("low", [P, T])
        u = sb("u", [P, K, T])
        dtin = sb("dtin", [DTR + 1, T])
        BC = sb("BC", [2 * DTR, T])
        Bhl = sb("Bhl", [P, 2, NQ * R], fr)
        Bst = sb("Bst", [P, NQ * R], fr)
        Bd = sb("Bd", [P, NQ, R, QT], fr)
        Cb = sb("Cb", [P, UNITS, UNIT])
        x1 = sb("x1", [P, TT, D])
        x1T = sb("x1T", [P, K, T])
        mids = sb("mids", [EM, T])
        gmT = sb("gmT", [P, TT, EM])
        gm = sb("gm", [EM, T])
        obuf = sb("obuf", [P, 2, D // 2])
        logits = sb("logits", [P, TT, E])
        beats = sb("beats", [P, 2, TT * E * E])
        gate = sb("gate", [P, 6, TT * E])
        B4 = obuf[:, :, :].rearrange("p a c -> p (a c)")

        sp = sb("sp", [P, 2, T])
        dt = sb("dt", [P, NDT, T])
        dtx = sb("dtx", [P, 2, T])
        Du = sb("Du", [P, 4, T])
        dxh = sb("dxh", [P, 2, TT * P], fr)
        dxl = sb("dxl", [P, 2, TT * P], fr)
        stack = sb("stack", [P, 2, NQ, P], fr)
        dA = sb("dA", [P, NDA, GB_ * HS * STEPS])
        h = sb("h", [P, NH, UNIT])
        hC = sb("hC", [P, NHC, UNIT])
        xres = sb("xres", [P, 2, TT, P])

        W2c = x1T[:, :, :].rearrange("p k t -> p (k t)")
        hCf = hC[:, :, :].rearrange("p a c -> p (a c)")
        xproj_n = hCf[0:2 * DTR, 0:D]
        F_n = hCf[0:EM + E, D:2 * D]
        expB_n = hCf[:, 2 * D:2 * D + K * EM].rearrange("p (k m) -> p k m", k=K)
        dtproj_n = hCf[:, 2 * D + K * EM:2 * D + K * EM + K * DTR].rearrange("p (k m) -> p k m", k=K)

        dBx = [ctx.enter_context(nc.psum_tensor(f"dBx{i}", [P, UNIT], fp32)) for i in range(2)]
        yp = [ctx.enter_context(nc.psum_tensor(f"yp{i}", [P, 512], fp32)) for i in range(2)]
        jb = [ctx.enter_context(nc.psum_tensor(f"jb{i}", [P, 512], fp32)) for i in range(2)]

        c_scratch = nc.dram_tensor("c_scratch", [GROUPS, UNITS, UNIT], fp32, kind="Internal").ap()

        s_idx, s_W, s_par, s_setw, s_W2c0, s_W2c1 = map(sem, ["idx_in", "W_in", "params_in", "setup_in", "W2c0_in", "W2c1_in"])
        s_W2 = [s_W2c0, s_W2c1]
        xin_in = [sem("xin0_in"), sem("xin1_in")]
        ga_in, gb_in, a2_in, b2_in = map(sem, ["ga_in", "gb_in", "a2_in", "b2_in"])
        stack_in = [sem("stack0_in"), sem("stack1_in")]
        xres_in = [sem("xres0_in"), sem("xres1_in")]
        cscr_out = sem("c_scratch_out")
        C_in = [sem(f"C{i}_in") for i in range(UNITS)]
        out_done = [sem("out0_done"), sem("out1_done")]
        s_cst, s_cstv, s_neg = map(sem, ["consts_made", "consts_made_dve", "negA_made"])
        set_full, set_taken, gt_full, gt_taken = map(sem, ["setup_full", "setup_taken", "gt_full", "gt_taken"])
        full, taken = {}, {}
        for _n in ["dtz", "x1T", "dtxT", "xT", "xr", "cond", "mid", "logit", "midT", "gm", "out", "xproj", "Bst", "A2T", "FB"]:
            full[_n], taken[_n] = sem(_n + "_full"), sem(_n + "_taken")
        per_group = {"dtz": K, "x1T": K, "dtxT": K, "xT": 4, "cond": K, "out": 4, "A2T": 2}
        h2_raw, h2_masked = sem("h2_raw"), sem("h2_masked")
        sp_step, dtx_made, Du_made, hi_made = map(sem, ["softplus_step", "dtx_made", "Du_made", "hi_made"])
        bc_made, b_step, Bd_made = map(sem, ["bc_made", "b_step", "Bd_made"])
        gate_step, gate_exp = sem("gate_step"), sem("gate_exp")
        dA_made, dBx_full, h_made, hC_made, sum_done, x1_made = map(
            sem, ["dA_made", "dBx_full", "h_made", "hC_made", "sum_done", "x1_made"])

        pe_passed, sp_passed = sem("pe_passed"), sem("sp_passed")

        block = ctx.enter_context(nc.Block())

        def wait(eng, s, value):
            if not isinstance(value, int) or value > 0:
                eng.wait_ge(s, value)

        def wait_alone(eng, passed, *waits):
            for s, v in zip(waits[::2], waits[1::2]):
                wait(eng, s, v)
                eng.sem_inc(passed, 1)

        def nth(name, G, i):
            return per_group.get(name, 1) * G + i + 1

        def group_of(name, G):
            return G - 1 if name in OF_PREVIOUS else G + 1 if name in OF_NEXT else G

        def jobs_of(G, j, un):
            first, last = isinstance(G, int) and G == 0, isinstance(G, int) and G == GROUPS - 1
            for name, i in JOBS[j, un]:
                if first and (name in OF_PREVIOUS or (name == "x1T" and i < 0)):
                    continue
                if last and (name in OF_NEXT or (name in ("dtz", "dtxT") and i >= K)):
                    continue
                yield name, i, group_of(name, G)

        def groups(eng, body):
            body(0)
            with eng.Fori(1, GROUPS - 1) as G:
                body(G)
            body(GROUPS - 1)

        @block.sync
        def _(sp_e):
            x_tok = x.rearrange("b s d -> (b s) d").rearrange("(g tt p) d -> g p tt d", tt=TT, p=P)
            out_tok = out.rearrange("b s d -> (b s) d").rearrange("(g tt p) d -> g p tt d", tt=TT, p=P)

            def of_group(ap, G):
                return ap[G] if isinstance(G, int) else ap[DynSlice(G, 1)].rearrange("o p tt d -> (o p) tt d")

            def load_x(G, i):
                wait(sp_e, taken["xT"], 4 * G + i - 1)
                sp_e.dma_start(xin[:, i % 2, :, :], of_group(x_tok, G)[:, :, 2 * P * i:2 * P * (i + 1)])\
                    .then_inc(xin_in[i % 2], 16)

            def load_adapters(G, which, table, dst, s):
                for b in range(GB_):
                    v = sp_e.value_load(idx[0:1, which, DynSlice(G * GB_ + b, 1)], min_val=0, max_val=table.shape[0] - 1)
                    sp_e.dma_start(dst(b), table[DynSlice(v, 1)].rearrange(
                        "o (k p) r -> p (o k) r" if table.shape[1] == D else "o r d -> (o r) d",
                        **({"p": P} if table.shape[1] == D else {}))).then_inc(s, 16)

            def load_lora(G):
                wait_alone(sp_e, sp_passed, full["xr"], G)
                load_adapters(G, 0, loraA, lambda b: GA[:, :, R * b:R * (b + 1)], ga_in)
                wait_alone(sp_e, sp_passed, full["cond"], K * G)
                load_adapters(G, 0, loraB, lambda b: GBA2[R * b:R * (b + 1), :], gb_in)

            def load_lora2(G):
                wait_alone(sp_e, sp_passed, full["A2T"], 2 * G)
                load_adapters(G, 1, lora2A, lambda b: GBA2[64 + R * b:64 + R * (b + 1), :], a2_in)
                wait_alone(sp_e, sp_passed, full["FB"], G)
                load_adapters(G, 1, lora2B, lambda b: B2g[:, :, R * b:R * (b + 1)], b2_in)

            def put_stack(t, par):
                wait_alone(sp_e, sp_passed, taken["dtxT"], t + 1, dBx_full, UNITS * (t - 1))
                for q, part in enumerate([dxh, dxh, dxl, dxl]):
                    for a in range(P // QT):
                        sp_e.dma_start(
                            stack[QT * q:QT * (q + 1), par, a:NQ:P // QT, :].bitcast(fp32),
                            part[QT * a:QT * (a + 1), par, :].bitcast(fp32).rearrange("p (tt d) -> p tt d", tt=TT))\
                            .then_inc(stack_in[par], 16)

            def load_xres(G, j, t):
                wait(sp_e, x1_made, t - 1)
                sp_e.dma_start(xres[:, j % 2, :, :], of_group(x_tok, G)[:, :, P * j:P * (j + 1)])\
                    .then_inc(xres_in[j % 2], 16)

            def put_c(G):
                wait(sp_e, bc_made, 3 * G + 3)
                dst = c_scratch[G] if isinstance(G, int) else c_scratch[DynSlice(G, 1)].rearrange("o a c -> (o a) c")
                for hh in range(2):
                    for p in range(2):
                        sp_e.dma_start(
                            dst[2 * hh + p].rearrange("(b n t) -> n b t", b=2, n=HS),
                            BC[48 + HS * hh:48 + HS * (hh + 1), p * P:(p + 1) * P].rearrange("n (b t) -> n b t", b=2))\
                            .then_inc(cscr_out, 16)

            def spread_c(G, un, of):
                if un == 0:
                    wait(sp_e, cscr_out, 64 * G + 64)
                wait(sp_e, hC_made, UNITS * K * G - UNITS + un + 1)
                src = c_scratch[G] if isinstance(G, int) else c_scratch[DynSlice(G, 1)].rearrange("o a c -> (o a) c")
                sp_e.dma_start(Cb[:, un, :], src[un:un + 1, :].to_broadcast([P, UNIT])).then_inc(C_in[un], 16)

            def store(G, i):
                wait(sp_e, taken["out"], 4 * G + i + 1)
                tt, half = i // 2, i % 2
                sp_e.dma_start(of_group(out_tok, G)[:, tt, half * 512:(half + 1) * 512], obuf[:, i % 2, :])\
                    .then_inc(out_done[i % 2], 16)

            sp_e.dma_start(idx[0:1, 0, :], ids1.rearrange("(o n) -> o n", o=1)).then_inc(s_idx, 16)
            sp_e.dma_start(idx[0:1, 1, :], ids2.rearrange("(o n) -> o n", o=1)).then_inc(s_idx, 16)
            load_x(0, 0)
            load_x(0, 1)
            sp_e.dma_start(xproj_n, xproj_w).then_inc(s_setw, 16)
            sp_e.dma_start(dtproj_n, dtproj_w.rearrange("(k p) r -> p k r", p=P)).then_inc(s_setw, 16)
            sp_e.dma_start(negA[:, :, :], A_log.rearrange("(k p) n -> p k n", p=P)).then_inc(s_par, 16)
            sp_e.dma_start(dtprojT[DTR:DTR + 1, :], dtproj_b.rearrange("(o n) -> o n", o=1)).then_inc(s_par, 16)
            for dst, src in ((Dsb, Dw), (bias_sb, bias2)):
                sp_e.dma_start(dst[:, :], src.rearrange("(k p) -> p k", p=P),
                               allow_slow_non_contiguous=True).then_inc(s_par, 16)
            for half in range(2):
                sp_e.dma_start(Wsb[:, :, half * 512:(half + 1) * 512],
                               W.rearrange("(k p) o -> p k o", p=P)[:, :, half * 512:(half + 1) * 512]).then_inc(s_W, 16)
                if half == 0:
                    sp_e.wait_ge(s_idx, 32)
                    load_x(0, 2)
                    load_x(0, 3)
                    load_lora(0)
            sp_e.dma_start(F_n[0:EM, :], expA.rearrange("e r d -> (e r) d")).then_inc(s_setw, 16)
            sp_e.dma_start(F_n[EM:EM + E, :], router_w).then_inc(s_setw, 16)
            for e in range(E):
                sp_e.dma_start(expB_n[:, :, R * e:R * (e + 1)], expB[e].rearrange("(k p) r -> p k r", p=P))\
                    .then_inc(s_setw, 16)
            put_c(0)
            for un in range(UNITS):
                spread_c(0, un, None)
            put_stack(0, 0)
            put_stack(1, 1)
            for k in range(K):
                wait(sp_e, gt_full, k - 1)
                sp_e.dma_start(W2c[:, (k % 2) * D:(k % 2 + 1) * D], W2[P * k:P * (k + 1), :]).then_inc(s_W2[k % 2], 16)

            def body(G):
                last = isinstance(G, int) and G == GROUPS - 1
                first = isinstance(G, int) and G == 0
                for j in range(K):
                    t = K * G + j
                    for un in range(UNITS):
                        if (j, un) == (0, 0) and not last:
                            load_x(G + 1, 0)
                            load_x(G + 1, 1)
                            load_lora(G + 1)
                        if (j, un) == (0, 3) and not last:
                            load_x(G + 1, 2)
                            load_x(G + 1, 3)
                        if un == 1:
                            load_xres(G, j, t)
                        if (j, un) == (3, 0):
                            load_lora2(G)
                        if (j, un) == (6, 1) and not last:
                            put_c(G + 1)
                        for name, i, g in jobs_of(G, j, un):
                            if name == "dtxT":
                                put_stack(K * g + i, i % 2)
                            if name == "out":
                                store(g, i)
                        if j == K - 1 and not last:
                            spread_c(G + 1, un, None)

            groups(sp_e, body)
            for i in range(4):
                store(GROUPS - 1, i)
            for s in out_done:
                sp_e.wait_ge(s, 16 * 2 * GROUPS)
            sp_e.wait_ge(cscr_out, 64 * GROUPS)

        @block.gpsimd
        def _(pool):
            made = 0

            def step(ins):
                nonlocal made
                made += 1
                ins.then_inc(s_cst, 1)
                pool.wait_ge(s_cst, made)

            def select(view, pattern, base, cm, op=ALU.not_equal, fill=1.0):
                step(pool.affine_select(out=view, in_=view, compare_op=op, fill=fill, base=base,
                                        pattern=pattern, channel_multiplier=cm))

            step(pool.memset(ident[:, :], 0.0))
            select(ident[:, :], [[-1, P]], 0, 1)
            step(pool.memset(own_batch[:, :], 1.0))
            for half in range(2):
                v = own_batch[64 * half:64 * half + 64, :].rearrange("p (b t) -> p b t", b=GB_)
                select(v, [[-R, GB_], [0, STEPS]], 0, 1, ALU.is_ge, 0.0)
                select(v, [[R, GB_], [0, STEPS]], R - 1, -1, ALU.is_ge, 0.0)
            step(pool.memset(diag32[:, :], 0.0))
            for q in range(4):
                select(diag32[QT * q:QT * (q + 1), :], [[-1, QT]], 0, 1)
            step(pool.memset(before[:, :, :], 1.0))
            select(before[:, :, :], [[1, E], [-1, E]], 0, 0, ALU.is_gt, 0.0)
            for q in range(4):
                step(pool.memset(use_hi[QT * q:QT * (q + 1), :], float(q % 2 == 0)))
                step(pool.memset(use_lo[QT * q:QT * (q + 1), :], float(q % 2 == 1)))
            step(pool.memset(dtin[DTR:DTR + 1, :], 1.0))

            def make_dtx(t, i):
                pool.wait_ge(taken["dtz"], t + 1)
                wait(pool, hi_made, t - 1)
                pool.tensor_tensor(dtx[:, i % 2, :], dt[:, i % NDT, :], u[:, i % K, :], ALU.mult).then_inc(dtx_made, 1)

            pool.wait_ge(taken["cond"], K)
            make_dtx(0, 0)
            make_dtx(1, 1)

            def body(G):
                for j in range(K):
                    for un in range(UNITS):
                        s = UNITS * (K * G + j) + un
                        pool.wait_ge(h_made, s + 1)
                        wait(pool, sum_done, s - NHC + 1)
                        if j == 0:
                            pool.wait_ge(C_in[un], 16 * G + 16)
                        pool.tensor_tensor(
                            hC[:, un % NHC, :].rearrange("p (n b t) -> p b n t", n=HS, b=2),
                            h[:, un % NH, :].rearrange("p (b n t) -> p b n t", n=HS, b=2),
                            Cb[:, un, :].rearrange("p (b n t) -> p b n t", n=HS, b=2), ALU.mult).then_inc(hC_made, 1)
                        if un == 2:
                            for name, i, g in jobs_of(G, j, 1):
                                if name == "dtz":
                                    if i == K:
                                        pool.wait_ge(taken["cond"], K * (g + 2))
                                    make_dtx(K * g + i, i)

            groups(pool, body)

        @block.scalar
        def _(act):
            def softplus_parts(t, i, bank):
                act.wait_ge(full["dtz"], t + 1)
                wait(act, taken["dtz"], t - 1)
                b = sp[:, i % 2, :]
                act.activation(b, jb[bank][:, 0:T], ACT.Abs).then_inc(sp_step, 1)
                act.wait_ge(sp_step, 3 * t + 1)
                act.activation(b, b, ACT.Exp, scale=-1.0).then_inc(sp_step, 1)
                act.wait_ge(sp_step, 3 * t + 2)
                act.activation(b, b, ACT.Ln, bias=1.0).then_inc(sp_step, 1)
                wait(act, sum_done, UNITS * (t - 3))
                act.activation(Du[:, i % 4, :], u[:, i % K, :], ACT.Copy, scale=Dsb[:, i % K:i % K + 1]).then_inc(Du_made, 1)

            def decays(G, j, half, part):
                q = 2 * (K * G + j) + half
                if part == 0:
                    act.wait_ge(taken["dtz"], K * G + j + 1)
                    wait(act, h_made, 2 * (q - NDA) + 2)
                for n in range(4 * part, 4 * part + 4):
                    act.activation(
                        dA[:, half % NDA, :].rearrange("p (b n t) -> p b n t", b=GB_, n=HS)[:, :, n, 1:STEPS],
                        dt[:, j % NDT, :].rearrange("p (b t) -> p b t", b=GB_)[:, :, 1:STEPS],
                        ACT.Exp, scale=negA[:, j, HS * half + n:HS * half + n + 1]).then_inc(dA_made, 1)

            def job(name, i, g, bank):
                psum = jb[bank]
                if name == "dtz":
                    return softplus_parts(K * g + i, i, bank)
                if name in ("xr", "logit", "midT", "out"):
                    return
                if name != "mid":
                    act.wait_ge(full[name], nth(name, g, i))
                if name == "dtxT":
                    t = K * g + i
                    wait(act, stack_in[i % 2], 256 * (K // 2 * g + i // 2))
                    act.activation(dxh[:, i % 2, :], psum[:, 0:T], ACT.Copy).then_inc(hi_made, 1)
                elif name == "x1T":
                    act.activation(x1T[:, i % K, :], psum[:, 0:T], ACT.Copy).then_inc(taken[name], 1)
                elif name == "xT":
                    act.activation(xT[:, 2 * i:2 * i + 2, :].rearrange("p k t -> p (k t)"), psum[:, :], ACT.Copy)\
                        .then_inc(taken[name], 1)
                elif name == "cond":
                    wait(act, dtx_made, K * (g - 1) + i + 1)
                    act.activation(u[:, i, :], psum[:, 0:T], ACT.Copy).then_inc(taken[name], 1)
                elif name == "xproj":
                    wait(act, cscr_out, 64 * g)
                    for s in out_done:
                        wait(act, s, 32 * (g - 1))
                    act.activation(dtin[0:DTR, :], psum[0:DTR, 0:T], ACT.Copy).then_inc(bc_made, 1)
                    act.activation(BC[DTR:2 * DTR, :], psum[DTR:2 * DTR, 0:T], ACT.Copy).then_inc(bc_made, 1)
                    act.activation(
                        B4[DTR:2 * DTR, :].rearrange("p (q a t) -> p q a t", q=NQ, a=4),
                        psum[DTR:2 * DTR, 0:T].rearrange("p (q t) -> p q t", q=NQ).unsqueeze(2)
                        .to_broadcast([DTR, NQ, 4, QT]), ACT.Copy).then_inc(bc_made, 1)
                elif name == "Bst":
                    act.activation(Bhl[:, 0, :], psum[:, 0:NQ * R], ACT.Copy).then_inc(b_step, 1)
                elif name == "A2T":
                    act.activation(GA2T[:, 4 * i:4 * i + 4, 64:P], psum[:, 0:256].rearrange("p (k m) -> p k m", k=4),
                                   ACT.Copy).then_inc(taken[name], 1)
                elif name == "FB":
                    act.activation(FB[64:P, :], psum[64:P, 0:EM + E], ACT.Copy).then_inc(taken[name], 1)
                elif name == "mid":
                    act.wait_ge(full["mid"], g + 1)
                    act.activation(mids[:, :], psum[0:EM, 0:T], ACT.Identity, bias=cmid[:, :]).then_inc(taken[name], 1)
                    act.wait_ge(gate_step, GATE_STEPS * g + 2)
                    act.activation(gate[:, 1, :], gate[:, 0, :], ACT.Exp).then_inc(gate_exp, 1)
                elif name == "gm":
                    act.activation(gm[:, :], psum[0:EM, 0:T], ACT.Copy).then_inc(taken[name], 1)

            act.wait_ge(s_par, 64)
            act.activation(negA[:, :, :], negA[:, :, :], ACT.Exp).then_inc(s_neg, 1)
            act.wait_ge(s_neg, 1)
            act.mul(negA[:, :, :], negA[:, :, :], -1.0).then_inc(s_neg, 1)
            act.wait_ge(s_neg, 2)
            act.wait_ge(s_cstv, 1)
            act.wait_ge(set_full, 1)
            act.activation(xprojT[:, :, :].rearrange("p k m -> p (k m)"), jb[0][:, :], ACT.Copy).then_inc(set_taken, 1)
            for i in range(2):
                act.wait_ge(set_full, 2 + i)
                act.activation(dtprojT[0:DTR, 512 * i:512 * (i + 1)], jb[1 - i][0:DTR, :], ACT.Copy).then_inc(set_taken, 1)
            for i in range(4):
                job("xT", i, 0, (i + 1) % 2)
            for o in range(K):
                job("cond", o, 0, o % 2)
            job("xproj", 0, 0, 0)
            job("dtz", 0, 0, 1)
            job("Bst", 0, 0, 0)
            job("dtz", 1, 0, 1)
            job("dtxT", 0, 0, 0)
            job("dtxT", 1, 0, 1)
            decays(0, 0, 0, 0)
            decays(0, 0, 0, 1)
            for i in range(2):
                act.wait_ge(set_full, 4 + i)
                act.activation(FT[:, 4 * i:4 * i + 4, :].rearrange("p k m -> p (k m)"), jb[i][:, 0:4 * (EM + E)], ACT.Copy)\
                    .then_inc(set_taken, 1)
            for i in range(2):
                act.wait_ge(set_full, 6 + i)
                act.activation(expBT[:, 512 * i:512 * (i + 1)], jb[i][0:EM, :], ACT.Copy).then_inc(set_taken, 1)
            act.wait_ge(gt_full, K)
            for i in range(2):
                v = yp[i][:, 0:4 * (EM + E)].rearrange("p (k m) -> p k m", k=4)
                act.activation(GA2T[:, 4 * i:4 * i + 4, 0:EM], v[:, :, 0:EM], ACT.Copy).then_inc(gt_taken, 1)
                act.activation(GTl[:, 4 * i:4 * i + 4, :], v[:, :, EM:EM + E], ACT.Copy).then_inc(gt_taken, 1)
            act.wait_ge(set_full, 8)
            act.activation(cmid[:, :], jb[0][0:EM, 0:1], ACT.Copy).then_inc(set_taken, 1)
            act.activation(clog[:, :], jb[0][:, 4:4 + E], ACT.Copy).then_inc(set_taken, 1)

            def body(G):
                last = isinstance(G, int) and G == GROUPS - 1
                for j in range(K):
                    for un in range(UNITS):
                        nj, nhalf = (j, 1) if un < 2 else (j + 1, 0)
                        if not (last and nj == K):
                            decays(G if nj < K else G + 1, nj % K, nhalf, un % 2)
                        for name, i, g in jobs_of(G, j, un):
                            job(name, i, g, BANK[name, i])

            groups(act, body)
            job("x1T", K - 2, GROUPS - 1, 0)
            job("x1T", K - 1, GROUPS - 1, 1)
            job("mid", 0, GROUPS - 1, 0)
            job("gm", 0, GROUPS - 1, 1)

        @block.vector
        def _(dve):
            def step_size(t, i, bank):
                dve.wait_ge(sp_step, 3 * t + 3)
                wait(dve, dA_made, R * (t - NDT + 1))
                dve.scalar_tensor_tensor(dt[:, i % NDT, :], jb[bank][:, 0:T], 0.0, sp[:, i % 2, :], ALU.max, ALU.add)\
                    .then_inc(taken["dtz"], 1)

            def add_residual(G, j, t):
                dve.wait_ge(sum_done, UNITS * (t + 1))
                dve.wait_ge(xres_in[j % 2], 16 * (K // 2 * G + j // 2 + 1))
                if j == 0:
                    wait(dve, taken["out"], 4 * G)
                dve.tensor_tensor(x1[:, :, P * j:P * (j + 1)], yp[j % 2][:, 0:T].rearrange("p (tt d) -> p tt d", tt=TT),
                                  xres[:, j % 2, :, :], ALU.add).then_inc(x1_made, 1)

            def b_diagonals(G, p):
                dve.wait_ge(b_step, 4 * G + 4)
                q = NQ // 2
                dve.tensor_tensor(
                    Bd[:, q * p:q * (p + 1), :, :].rearrange("p q n t -> p (q n) t"),
                    Bst[:, q * R * p:q * R * (p + 1)].bitcast(fp32).unsqueeze(2).to_broadcast([P, q * R, QT]),
                    diag32[:, :].unsqueeze(1).to_broadcast([P, q * R, QT]), ALU.mult).then_inc(Bd_made, 1)

            def gating(g, bank):
                n = 0

                def link(ins):
                    nonlocal n
                    n += 1
                    ins.then_inc(gate_step, 1)
                    dve.wait_ge(gate_step, GATE_STEPS * g + n)

                def te(i):
                    return gate[:, i, :].rearrange("p (a e) -> p a e", a=TT)

                def ee(i):
                    return beats[:, i, :].rearrange("p (a e f) -> p (a e) f", e=E, f=E)

                shape = [P, TT, E]
                top = gate[:, 2, 0:TT]
                link(dve.tensor_reduce(top, logits[:, :, :], AX.X, ALU.max))
                link(dve.tensor_tensor(te(0), logits[:, :, :], top.unsqueeze(2).to_broadcast(shape), ALU.subtract))
                for tt in range(TT):
                    other = logits[:, tt, :].unsqueeze(1).to_broadcast([P, E, E])
                    own = logits[:, tt, :].unsqueeze(2).to_broadcast([P, E, E])
                    dve.tensor_tensor(ee(0)[:, E * tt:E * (tt + 1), :], other, own, ALU.is_gt)
                    dve.tensor_tensor(ee(1)[:, E * tt:E * (tt + 1), :], other, own, ALU.is_equal)
                link(dve.tensor_copy(gate[:, 5, 0:1], use_hi[:, :]))
                for tt in range(TT):
                    last = dve.tensor_tensor(ee(1)[:, E * tt:E * (tt + 1), :], ee(1)[:, E * tt:E * (tt + 1), :],
                                             before[:, :, :], ALU.mult)
                link(last)
                link(dve.tensor_tensor(beats[:, 0, :], beats[:, 0, :], beats[:, 1, :], ALU.add))
                link(dve.tensor_reduce(gate[:, 3, :], ee(0), AX.X, ALU.add))
                dve.wait_ge(gate_exp, g + 1)
                link(dve.scalar_tensor_tensor(gate[:, 1, :], gate[:, 3, :], 1.5, gate[:, 1, :], ALU.is_lt, ALU.mult))
                link(dve.tensor_reduce(gate[:, 2, 0:TT], te(1), AX.X, ALU.add))
                link(dve.reciprocal(gate[:, 3, 0:TT], gate[:, 2, 0:TT]))
                link(dve.scalar_tensor_tensor(te(4), te(1), LORA2_SCALE, gate[:, 3, 0:TT].unsqueeze(2).to_broadcast(shape),
                                              ALU.mult, ALU.mult))
                assert n == GATE_STEPS

            def job(name, i, g, bank):
                psum = jb[bank]
                if name == "dtz":
                    return step_size(K * g + i, i, bank)
                if name == "dtxT":
                    t = K * g + i
                    dve.wait_ge(hi_made, t + 1)
                    dve.tensor_tensor(dxl[:, i % 2, :], psum[:, 0:T], dxh[:, i % 2, :].bitcast(fp32), ALU.subtract)\
                        .then_inc(taken[name], 1)
                elif name == "xr":
                    dve.wait_ge(full[name], g + 1)
                    dve.tensor_tensor(low[0:64, :], psum[0:64, 0:T], own_batch[0:64, :], ALU.mult).then_inc(taken[name], 1)
                elif name == "Bst":
                    dve.wait_ge(b_step, 4 * g + 1)
                    dve.tensor_tensor(Bhl[:, 1, :], psum[:, 0:NQ * R], Bhl[:, 0, :].bitcast(fp32), ALU.subtract)\
                        .then_inc(b_step, 1)
                    dve.wait_ge(b_step, 4 * g + 2)
                    dve.tensor_scalar(Bst[:, :], Bhl[:, 0, :].bitcast(fp32), use_hi[:, :], None, ALU.mult).then_inc(b_step, 1)
                    dve.wait_ge(b_step, 4 * g + 3)
                    dve.scalar_tensor_tensor(Bst[:, :], Bhl[:, 1, :].bitcast(fp32), use_lo[:, :], Bst[:, :].bitcast(fp32),
                                             ALU.mult, ALU.add).then_inc(b_step, 1)
                elif name == "mid":
                    dve.wait_ge(h2_raw, g + 1)
                    dve.tensor_tensor(low[64:P, :], psum[64:P, 0:T], own_batch[64:P, :], ALU.mult).then_inc(h2_masked, 1)
                elif name == "logit":
                    dve.wait_ge(full[name], g + 1)
                    dve.tensor_tensor(logits[:, :, :], psum[:, 0:TT * E].rearrange("p (a e) -> p a e", a=TT),
                                      clog[:, :].unsqueeze(1).to_broadcast([P, TT, E]), ALU.add).then_inc(taken[name], 1)
                    dve.wait_ge(taken[name], g + 1)
                    gating(g, bank)
                elif name == "midT":
                    dve.wait_ge(full[name], g + 1)
                    dve.tensor_tensor(
                        gmT[:, :, :].rearrange("p a (e r) -> p (a e) r", e=E),
                        psum[:, 0:TT * EM].rearrange("p (a r) -> p a r", r=R),
                        gate[:, 4, :].unsqueeze(2).to_broadcast([P, TT * E, R]), ALU.mult).then_inc(taken[name], 1)
                elif name == "out":
                    dve.wait_ge(full[name], 4 * g + i + 1)
                    if i >= 2:
                        wait(dve, out_done[i % 2], 16 * (2 * g + 1))
                    tt, half = i // 2, i % 2
                    dve.tensor_tensor(obuf[:, i % 2, :], psum[:, :], x1[:, tt, half * 512:(half + 1) * 512], ALU.add)\
                        .then_inc(taken[name], 1)

            for i in range(NDA):
                last = dve.memset(dA[:, i, :].rearrange("p (b n t) -> p (b n) t", b=GB_, n=HS)[:, :, 0:1], 0.0)
            last.then_inc(s_cstv, 1)
            dve.wait_ge(s_cst, CONSTS)
            job("xr", 0, 0, 1)
            job("dtz", 0, 0, 1)
            job("Bst", 0, 0, 0)
            b_diagonals(0, 0)
            b_diagonals(0, 1)
            job("dtz", 1, 0, 1)
            job("dtxT", 0, 0, 0)
            job("dtxT", 1, 0, 1)

            def body(G):
                first, final = (isinstance(G, int) and G == g for g in (0, GROUPS - 1))
                for j in range(K):
                    t = K * G + j
                    for un in range(UNITS):
                        s, half, p = UNITS * t + un, un // 2, un % 2
                        dve.wait_ge(dBx_full, s + 1)
                        dve.wait_ge(dA_made, R * t + HS * (half + 1))
                        wait(dve, hC_made, s - NH + 1)
                        dve.tensor_tensor_scan(h[:, un % NH, :], dA[:, half % NDA, UNIT * p:UNIT * (p + 1)], dBx[un % 2][:, :],
                                               0.0, ALU.mult, ALU.add).then_inc(h_made, 1)
                        if j == K - 1 and half == 1 and not final:
                            b_diagonals(G + 1, p)
                        if un == 2:
                            if j >= 2:
                                add_residual(G, j - 2, t - 2)
                            elif not first:
                                add_residual(G - 1, j - 2 + K, t - 2)
                        for name, i, g in jobs_of(G, j, un):
                            job(name, i, g, BANK[name, i])

            groups(dve, body)
            add_residual(GROUPS - 1, K - 2, K * GROUPS - 2)
            add_residual(GROUPS - 1, K - 1, K * GROUPS - 1)
            job("mid", 0, GROUPS - 1, 0)
            job("logit", 0, GROUPS - 1, 1)
            job("midT", 0, GROUPS - 1, 0)
            for i in range(4):
                job("out", i, GROUPS - 1, i % 2)

        @block.tensor
        def _(pe):
            tenant = {}

            def mm(o, lhsT, rhs, start, stop, **kw):
                return pe.matmul(o, lhsT, rhs, start=start, stop=stop, **kw)

            def tr(o, in_, n, first=0):
                return pe.matmul(o, in_, ident[first:first + n, first:first + n], is_transpose=True, start=True, stop=True)

            def job(name, i, g, bank):
                operand = {"Bst": (bc_made, 3 * g + 3), "A2T": (a2_in, 64 * g + 64),
                           "midT": (taken["mid"], g + 1), "gm": (taken["midT"], g + 1)}.get(name, ())
                if operand:
                    wait_alone(pe, pe_passed, *tenant.get(bank, ()), *operand)
                elif bank in tenant:
                    wait(pe, *tenant[bank])
                tenant[bank] = (taken[name], nth(name, g, i))
                psum = jb[bank]
                if name == "dtz":
                    pe.wait_ge(bc_made, 3 * (g if i < K else g + 1) + 1)
                    last = mm(psum[:, 0:T], dtprojT[:, P * (i % K):P * (i % K + 1)], dtin[:, :], True, True)
                elif name == "dtxT":
                    pe.wait_ge(dtx_made, K * g + i + 1)
                    for tt in range(TT):
                        last = tr(psum[:, P * tt:P * (tt + 1)], dtx[:, i % 2, P * tt:P * (tt + 1)], P)
                elif name == "x1T":
                    pe.wait_ge(x1_made, K * g + i + 1)
                    for tt in range(TT):
                        last = tr(psum[:, P * tt:P * (tt + 1)], x1[:, tt, P * (i % K):P * (i % K + 1)], P)
                elif name == "xT":
                    pe.wait_ge(xin_in[i % 2], 16 * (2 * g + i // 2 + 1))
                    for a in range(2):
                        for tt in range(TT):
                            c = (a * TT + tt) * P
                            last = tr(psum[:, c:c + P], xin[:, i % 2, tt, P * a:P * (a + 1)], P)
                elif name == "xr":
                    pe.wait_ge(taken["xT"], 4 * g + 4)
                    pe.wait_ge(ga_in, 64 * g + 64)
                    for k in range(K):
                        last = mm(psum[0:64, 0:T], GA[:, k, :], xT[:, k, :], k == 0, k == K - 1)
                elif name == "cond":
                    for k in range(K):
                        mm(psum[:, 0:T], Wsb[:, k, P * i:P * (i + 1)], xT[:, k, :], k == 0, False)
                    if i == 0:
                        pe.wait_ge(taken["xr"], g + 1)
                        pe.wait_ge(gb_in, 64 * g + 64)
                    last = mm(psum[:, 0:T], GBA2[0:64, P * i:P * (i + 1)], low[0:64, :], False, True)
                elif name == "xproj":
                    pe.wait_ge(taken["cond"], K * g + K)
                    for k in range(K):
                        last = mm(psum[0:2 * DTR, 0:T], xprojT[:, k, :], u[:, k, :], k == 0, k == K - 1)
                    tenant[bank] = (bc_made, 3 * g + 3)
                elif name == "Bst":
                    for q in range(NQ):
                        last = pe.matmul(psum[:, R * q:R * (q + 1)], B4[DTR:DTR + R, P * q:P * (q + 1)],
                                         ident[DTR:DTR + R, DTR:DTR + R], is_transpose=True, start=True, stop=True)
                    tenant[bank] = (b_step, 4 * g + 2)
                elif name == "A2T":
                    for a in range(4):
                        k = 4 * i + a
                        last = tr(psum[:, 64 * a:64 * (a + 1)], GBA2[64:P, P * k:P * (k + 1)], 64, 64)
                elif name == "FB":
                    pe.wait_ge(b2_in, 64 * g + 64)
                    for k in range(K):
                        last = mm(psum[64:P, 0:EM + E], B2g[:, k, :], FT[:, k, :], k == 0, k == K - 1)
                elif name == "mid":
                    pe.wait_ge(taken["x1T"], K * g + K)
                    pe.wait_ge(taken["A2T"], 2 * g + 2)
                    for k in range(K):
                        last = mm(psum[:, 0:T], GA2T[:, k, :], x1T[:, k, :], k == 0, k == K - 1)
                    last.then_inc(h2_raw, 1)
                    return
                elif name == "logit":
                    pe.wait_ge(taken["FB"], g + 1)
                    for tt in range(TT):
                        for k in range(K):
                            mm(psum[:, E * tt:E * (tt + 1)], x1T[:, k, P * tt:P * (tt + 1)], GTl[:, k, :],
                               k == 0, False, skip_group_check=True) if tt == 0 or k else \
                                mm(psum[:, E * tt:E * (tt + 1)], x1T[:, k, P * tt:P * (tt + 1)], GTl[:, k, :],
                                   False, False, skip_group_check=True)
                    wait_alone(pe, pe_passed, h2_masked, g + 1)
                    mb = 1 - bank
                    mm(jb[mb][0:EM, 0:T], FB[64:P, 0:EM], low[64:P, :], False, True, skip_group_check=True)\
                        .then_inc(full["mid"], 1)
                    for tt in range(TT):
                        last = mm(psum[:, E * tt:E * (tt + 1)], low[64:P, P * tt:P * (tt + 1)], FB[64:P, EM:EM + E],
                                  False, True, skip_group_check=True)
                elif name == "midT":
                    for tt in range(TT):
                        last = tr(psum[:, EM * tt:EM * (tt + 1)], mids[:, P * tt:P * (tt + 1)], EM)
                elif name == "gm":
                    for tt in range(TT):
                        last = tr(psum[0:EM, P * tt:P * (tt + 1)], gmT[:, tt, :], P)
                elif name == "out":
                    pe.wait_ge(taken["gm"], g + 1)
                    tt, half = i // 2, i % 2
                    last = mm(psum[:, :], gm[:, P * tt:P * (tt + 1)], expBT[:, half * 512:(half + 1) * 512], True, True)
                last.then_inc(full[name], 1)

            def b_times_dtx(G, j, un):
                t = K * G + j
                s, half, p = UNITS * t + un, un // 2, un % 2
                if un == 0:
                    pe.wait_ge(stack_in[j % 2], 256 * (K // 2 * G + j // 2 + 1))
                if j == 0 and half == 0:
                    pe.wait_ge(Bd_made, 2 * G + p + 1)
                wait(pe, h_made, s - 1)
                for b in range(2):
                    for a in range(2):
                        q = 4 * p + 2 * b + a
                        o = dBx[un % 2][:, 512 * b:512 * (b + 1)].rearrange("p (n t) -> p n t", n=HS)[:, :, QT * a:QT * (a + 1)]
                        last = mm(o, stack[:, j % 2, q, :],
                                  Bd[:, q, HS * half:HS * (half + 1), :].rearrange("p n t -> p (n t)"),
                                  True, True, skip_group_check=True)
                last.then_inc(dBx_full, 1)

            def sum_states(G, j, un):
                t = K * G + j
                half, p = un // 2, un % 2
                pe.wait_ge(hC_made, UNITS * t + un + 1)
                if un == 0:
                    wait(pe, x1_made, t - 1)
                y = yp[j % 2][:, P * p:P * (p + 1)]
                for n in range(HS):
                    last = pe.matmul(y, hC[:, un % NHC, P * n:P * (n + 1)], ident[:, :], is_transpose=True,
                                     start=un == 0 and n == 0, stop=False, skip_group_check=True)
                if half == 1:
                    if p == 0:
                        pe.wait_ge(Du_made, t + 1)
                    last = pe.matmul(y, Du[:, j % 4, P * p:P * (p + 1)], ident[:, :], is_transpose=True,
                                     start=False, stop=True, skip_group_check=True)
                last.then_inc(sum_done, 1)

            def set_up(bank, n):
                wait(pe, set_taken, n)

            pe.wait_ge(s_cst, CONSTS)
            pe.wait_ge(s_setw, 32)
            for k in range(K):
                last = tr(jb[0][:, 64 * k:64 * (k + 1)], xproj_n[:, P * k:P * (k + 1)], 64)
            last.then_inc(set_full, 1)
            for i in range(2):
                set_up(1 - i, i)
                for a in range(4):
                    last = tr(jb[1 - i][0:DTR, P * a:P * (a + 1)], dtproj_n[:, 4 * i + a, :], P)
                last.then_inc(set_full, 1)
            tenant[1], tenant[0] = (set_taken, 2), (set_taken, 3)
            for i in range(4):
                job("xT", i, 0, (i + 1) % 2)
            job("xr", 0, 0, 1)
            pe.wait_ge(s_W, 16)
            for o in range(K):
                if o == 4:
                    pe.wait_ge(s_W, 32)
                job("cond", o, 0, o % 2)
            pe.wait_ge(s_par, 64)
            job("xproj", 0, 0, 0)
            job("dtz", 0, 0, 1)
            job("Bst", 0, 0, 0)
            job("dtz", 1, 0, 1)
            job("dtxT", 0, 0, 0)
            job("dtxT", 1, 0, 1)
            pe.wait_ge(s_setw, 128)
            n = EM + E
            for i in range(2):
                wait(pe, taken["dtxT"], i + 1)
                for a in range(4):
                    last = tr(jb[i][:, n * a:n * (a + 1)], F_n[:, P * (4 * i + a):P * (4 * i + a + 1)], n)
                last.then_inc(set_full, 1)
            for i in range(2):
                set_up(i, 4 + i)
                for a in range(4):
                    last = tr(jb[i][0:EM, P * a:P * (a + 1)], expB_n[:, 4 * i + a, :], P)
                last.then_inc(set_full, 1)
            for k in range(K):
                pe.wait_ge(s_W2[k % 2], 16 * (k // 2 + 1))
                for c in range(K):
                    last = mm(yp[c // 4][:, n * (c % 4):n * (c % 4 + 1)],
                              W2c[:, (k % 2) * D + P * c:(k % 2) * D + P * (c + 1)], FT[:, k, :],
                              k == 0 and c % 4 == 0, k == K - 1, skip_group_check=True)
                last.then_inc(gt_full, 1)
            set_up(0, 6)
            for k in range(K):
                mm(jb[0][0:EM, 0:1], FT[:, k, 0:EM], bias_sb[:, k:k + 1], k == 0, k == K - 1, skip_group_check=True)
            for k in range(K):
                last = mm(jb[0][:, 4:4 + E], bias_sb[:, k:k + 1].to_broadcast([P, P]), FT[:, k, EM:n],
                          False, k == K - 1, skip_group_check=True)
            last.then_inc(set_full, 1)
            pe.wait_ge(gt_taken, 4)
            pe.wait_ge(set_taken, 9)

            def body(G):
                first = isinstance(G, int) and G == 0
                tenant.clear()
                if not first:
                    tenant[BANK["x1T", K - 3]] = (taken["x1T"], K * (G - 1) + K - 2)
                    tenant[BANK["dtxT", K + 1]] = (taken["dtxT"], K * (G - 1) + K + 2)
                for j in range(K):
                    for un in range(UNITS):
                        b_times_dtx(G, j, un)
                        back = UNITS * j + un - LAG
                        if back >= 0:
                            sum_states(G, back // UNITS, back % UNITS)
                        elif not first:
                            sum_states(G - 1, K - 1, back % UNITS)
                        for name, i, g in jobs_of(G, j, un):
                            job(name, i, g, BANK[name, i])

            groups(pe, body)
            G = GROUPS - 1
            for un in range(UNITS - LAG, UNITS):
                sum_states(G, K - 1, un)
            job("x1T", K - 2, G, 0)
            job("x1T", K - 1, G, 1)
            job("mid", 0, G, 0)
            job("logit", 0, G, 1)
            job("midT", 0, G, 0)
            job("gm", 0, G, 1)
            for i in range(4):
                job("out", i, G, i % 2)


GATE_STEPS = 10
CONSTS = 23

_INS = ['x', 'itok_B_0_15', 'itok_B_6_15', 'L0_cond_W', 'L0_cond_lora_A', 'L0_cond_lora_B', 'L0_attn_A_log', 'L0_attn_D',
        'L0_attn_x_proj_w', 'L0_attn_dt_proj_w', 'L0_attn_dt_proj_b', 'L0_cond2_base_weight', 'L0_cond2_base_bias',
        'L0_cond2_lora_A_w', 'L0_cond2_lora_B_w', 'L0_ffn_router_w', 'L0_ffn_A', 'L0_ffn_B']


def kernel(**inputs):
    import numpy as _np
    import concourse.bacc as _bacc
    from concourse import mybir as _mybir
    from concourse.bass_utils import run_bass_kernel_spmd as _run

    nc = _bacc.Bacc("TRN2", target_bir_lowering=False, num_devices=1)
    arrays, args = {}, []
    for name in _INS:
        a = _np.ascontiguousarray(inputs[name])
        arrays[f"in_{name}"] = a
        args.append(nc.dram_tensor(f"in_{name}", a.shape, _mybir.dt.from_np(a.dtype), kind="ExternalInput").ap())
    o = nc.dram_tensor("out_0", (BATCHES, STEPS, D), _mybir.dt.float32, kind="ExternalOutput").ap()
    layer_kernel(nc, *args, o)
    r = _run(nc, [arrays], core_ids=[0])
    return r.results[0]["out_0"]
```

```python
import concourse.bass as bass
from concourse import mybir
from contextlib import ExitStack

P = 128
BATCHES, STEPS, D = 32, 64, 1024
R = 16
GROUPS = 8
GB_ = BATCHES // GROUPS
T = GB_ * STEPS
TT = T // P
K = D // P
DTR = 32
E = 4
EM = E * R
HS = R // 2
UNIT = HS * P
UNITS = 4
QT = 32
NQ = T // QT
LAG = 3
NDA, NH, NHC, NDT = 2, 2, 4, 4
LORA2_SCALE = 16.0 / 16.0 ** 0.5

JOBS = {(j, u): [] for j in range(K) for u in range(UNITS)}
for _j in range(K):
    if _j == 3:
        JOBS[_j, 0].append(("x1T", 0))
    if _j not in (1, 2):
        JOBS[_j, 0].append(("x1T", _j - 2))
    if _j != 7:
        JOBS[_j, 0].append(("dtxT", _j + 1))
    if _j != 6:
        JOBS[_j, 0].append(("dtz", _j + 2))
JOBS[0, 1] += [("xT", 0), ("xT", 1)]
JOBS[0, 2] += [("xT", 2), ("xT", 3)]
JOBS[0, 3] += [("xr", 0), ("x1T", -1)]
JOBS[1, 0] += [("mid", 0)]
JOBS[1, 1] += [("h2T", 0)]
JOBS[1, 2] += [("mid2", 0), ("cond", 0)]
JOBS[1, 3] += [("gate", 0)]
JOBS[2, 0] += [("gm", 0)]
JOBS[2, 1] += [("out", 0), ("out", 1)]
JOBS[2, 2] += [("out", 2), ("out", 3)]
for _o, _at in enumerate([(2, 3), (3, 1), (3, 3), (4, 1), (4, 3), (5, 1), (5, 3)]):
    JOBS[_at] += [("cond", _o + 1)]
JOBS[6, 1] += [("xproj", 0)]
JOBS[6, 2] += [("dtz", K), ("Bst", 0)]
JOBS[7, 0] += [("dtxT", K)]
JOBS[7, 2] += [("A2T", 0), ("A2T", 1)]
JOBS[7, 3] += [("FB", 0)]
LATE = {("dtz", i) for i in range(K + 2) if i != K} | {("Bst", 0)}
BANK, LAST_JOB = {}, {}
_b = 1
for _at in sorted(JOBS):
    for _job in JOBS[_at]:
        if _job[0] not in ("mid2", "gate"):
            _b = _b if _job == ("cond", 0) else 1 - _b
            BANK[_job], LAST_JOB[_b] = _b, _job
BANK["mid2", 0] = BANK["gate", 0] = BANK["mid", 0]
OF_PREVIOUS = {"mid", "h2T", "mid2", "gate", "gm", "out"}
OF_NEXT = {"xT", "xr", "cond", "xproj", "Bst"}


def layer_kernel(nc, x, ids1, ids2, W, loraA, loraB, A_log, Dw, xproj_w, dtproj_w, dtproj_b,
                 W2, bias2, lora2A, lora2B, router_w, expA, expB, out):
    fp32, fr, i32 = mybir.dt.float32, mybir.dt.float32r, mybir.dt.int32
    ALU, ACT, AX = mybir.AluOpType, mybir.ActivationFunctionType, mybir.AxisListType
    DynSlice = bass.DynSlice

    ctx = ExitStack()
    with ctx:
        def sb(name, shape, dt=fp32):
            return ctx.enter_context(nc.sbuf_tensor(name, shape, dt))

        def sem(name):
            return ctx.enter_context(nc.semaphore(name))

        ident = sb("ident", [P, P])
        diag32 = sb("diag32", [P, QT])
        own_batch = sb("own_batch", [GB_ * R, T])
        own_rank = sb("own_rank", [P, TT, GB_ * R])
        use_hi = sb("use_hi", [P, 1])
        use_lo = sb("use_lo", [P, 1])
        before = sb("before", [P, E, E])
        idx = sb("idx", [1, 2, BATCHES], i32)
        Wsb = sb("Wsb", [P, K, D])
        negA = sb("negA", [P, K, R])
        Dsb = sb("Dsb", [P, K])
        xprojT = sb("xprojT", [P, K, 2 * DTR])
        dtprojT = sb("dtprojT", [DTR + 1, D])
        FT = sb("FT", [P, K, EM + E])
        G2 = sb("G2", [P, K, EM + E + GB_ * R])
        cF = sb("cF", [P, EM + E])
        bias_sb = sb("bias_sb", [P, K])
        expBT = sb("expBT", [EM, D])

        xin = sb("xin", [P, 4, TT, 2 * P])
        xT = sb("xT", [P, K, T])
        GA = sb("GA", [P, K, GB_ * R])
        GBA2 = sb("GBA2", [P, D])
        B2g = sb("B2g", [P, K, GB_ * R])
        FB = sb("FB", [P, EM + E])
        low = sb("low", [P, T])
        u = sb("u", [P, K, T])
        dtin = sb("dtin", [DTR + 1, T])
        BC = sb("BC", [2 * DTR, T])
        Bhl = sb("Bhl", [P, 2, NQ * R], fr)
        Bst = sb("Bst", [P, NQ * R], fr)
        Bd = sb("Bd", [P, NQ, R, QT], fr)
        Cb = sb("Cb", [P, UNITS, UNIT])
        x1 = sb("x1", [P, TT, D])
        x1T = sb("x1T", [P, K, T])
        h2m = sb("h2m", [P, TT, GB_ * R])
        mids = sb("mids", [P, TT, EM + E])
        gmT = sb("gmT", [P, TT, EM])
        gm = sb("gm", [EM, T])
        obuf = sb("obuf", [P, 2, D // 2])
        beats = sb("beats", [P, 2, TT * E * E])
        gate = sb("gate", [P, 6, TT * E])
        B4 = obuf[:, :, :].rearrange("p a c -> p (a c)")

        sp = sb("sp", [P, T])
        dt = sb("dt", [P, NDT, T])
        dtx = sb("dtx", [P, T])
        Du = sb("Du", [P, 4, T])
        parts = sb("parts", [P, 2, T], fr)
        stack = sb("stack", [P, 2, P // QT, TT, P], fr)
        dA = sb("dA", [P, NDA, GB_ * HS * STEPS])
        h = sb("h", [P, NH, UNIT])
        hC = sb("hC", [P, NHC, UNIT])
        xres = sb("xres", [P, 2, TT, P])

        W2c = [x1T[:, 0:4, :].rearrange("p k t -> p (k t)"), x1T[:, 4:8, :].rearrange("p k t -> p (k t)"),
               x1[:, 0, :], x1[:, 1, :]]
        G_n = h[0:EM + E, 1, :]
        hCf = hC[:, :, :].rearrange("p a c -> p (a c)")
        xproj_n = hCf[0:2 * DTR, 0:D]
        F_n = hCf[0:EM + E, D:2 * D]
        expB_n = hCf[:, 2 * D:2 * D + K * EM].rearrange("p (k m) -> p k m", k=K)
        dtproj_n = hCf[:, 2 * D + K * EM:2 * D + K * EM + K * DTR].rearrange("p (k m) -> p k m", k=K)

        dBx = [ctx.enter_context(nc.psum_tensor(f"dBx{i}", [P, UNIT], fp32)) for i in range(2)]
        yp = [ctx.enter_context(nc.psum_tensor(f"yp{i}", [P, 512], fp32)) for i in range(2)]
        jb = [ctx.enter_context(nc.psum_tensor(f"jb{i}", [P, 512], fp32)) for i in range(2)]

        parts_scratch = nc.dram_tensor("parts_scratch", [2, 2, QT, P // QT, T], fp32, kind="Internal").ap()
        c_scratch = nc.dram_tensor("c_scratch", [GROUPS, UNITS, UNIT], fp32, kind="Internal").ap()

        s_idx, s_W0, s_W1, s_par, s_setw, s_F = map(sem, ["idx_in", "W0_in", "W1_in", "params_in", "proj_in", "F_in"])
        s_W2 = [sem(f"W2c{i}_in") for i in range(4)]
        xin_in = [sem(f"xin{i}_in") for i in range(4)]
        ga_in, gb_in, a2_in, b2_in = map(sem, ["ga_in", "gb_in", "a2_in", "b2_in"])
        stack_in = [sem("stack0_in"), sem("stack1_in")]
        xres_in = [sem("xres0_in"), sem("xres1_in")]
        parts_out = sem("parts_out")
        cscr_out = sem("c_scratch_out")
        C_in = [sem(f"C{i}_in") for i in range(UNITS)]
        out_done = [sem("out0_done"), sem("out1_done")]
        s_cst, s_cstv, s_neg = map(sem, ["consts_made", "consts_made_dve", "negA_made"])
        set_full, set_taken, gt_full, gt_taken = map(sem, ["setup_full", "setup_taken", "gt_full", "gt_taken"])
        full, taken = {}, {}
        for _n in ["dtz", "x1T", "dtxT", "xT", "xr", "cond", "mid", "h2T", "gm", "out", "xproj", "Bst", "A2T", "FB"]:
            full[_n], taken[_n] = sem(_n + "_full"), sem(_n + "_taken")
        per_group = {"dtz": K, "x1T": K, "dtxT": K, "xT": 4, "cond": K, "out": 4, "A2T": 2}
        h2_raw, h2_masked, gated = sem("h2_raw"), sem("h2_masked"), sem("gated")
        sp_step, dtx_made, Du_made, hi_made = map(sem, ["softplus_step", "dtx_made", "Du_made", "hi_made"])
        bc_made, b_step, Bd_made = map(sem, ["bc_made", "b_step", "Bd_made"])
        gate_step, gate_exp = sem("gate_step"), sem("gate_exp")
        dA_made, dBx_full, h_made, hC_made, sum_done, x1_made = map(
            sem, ["dA_made", "dBx_full", "h_made", "hC_made", "sum_done", "x1_made"])

        pe_passed, sp_passed = sem("pe_passed"), sem("sp_passed")

        block = ctx.enter_context(nc.Block())

        def wait(eng, s, value):
            if not isinstance(value, int) or value > 0:
                eng.wait_ge(s, value)

        def wait_alone(eng, passed, *waits):
            for s, v in zip(waits[::2], waits[1::2]):
                wait(eng, s, v)
                eng.sem_inc(passed, 1)

        def nth(name, G, i):
            return per_group.get(name, 1) * G + i + 1

        def group_of(name, G):
            return G - 1 if name in OF_PREVIOUS else G + 1 if name in OF_NEXT else G

        def jobs_of(G, j, un):
            first, last = isinstance(G, int) and G == 0, isinstance(G, int) and G == GROUPS - 1
            for name, i in JOBS[j, un]:
                if first and (name in OF_PREVIOUS or (name == "x1T" and i < 0)):
                    continue
                if last and (name in OF_NEXT or (name in ("dtz", "dtxT") and i >= K)):
                    continue
                yield name, i, group_of(name, G)

        def groups(eng, body):
            body(0)
            with eng.Fori(1, GROUPS - 1) as G:
                body(G)
            body(GROUPS - 1)

        x_tok = x.rearrange("b s d -> (b s) d").rearrange("(g tt p) d -> g p tt d", tt=TT, p=P)
        out_tok = out.rearrange("b s d -> (b s) d").rearrange("(g tt p) d -> g p tt d", tt=TT, p=P)

        def of_group(ap, G):
            return ap[G] if isinstance(G, int) else ap[DynSlice(G, 1)].rearrange("o p tt d -> (o p) tt d")

        def load_x(eng, G, i):
            wait(eng, taken["xT"], 4 * (G - 1) + i + 1)
            eng.dma_start(xin[:, i, :, :], of_group(x_tok, G)[:, :, 2 * P * i:2 * P * (i + 1)]).then_inc(xin_in[i], 16)

        @block.sync
        def _(sp_e):

            def load_adapters(G, which, table, dst, s):
                for b in range(GB_):
                    v = sp_e.value_load(idx[0:1, which, DynSlice(G * GB_ + b, 1)], min_val=0, max_val=table.shape[0] - 1)
                    sp_e.dma_start(dst(b), table[DynSlice(v, 1)].rearrange(
                        "o (k p) r -> p (o k) r" if table.shape[1] == D else "o r d -> (o r) d",
                        **({"p": P} if table.shape[1] == D else {}))).then_inc(s, 16)

            def load_lora_a(G):
                wait_alone(sp_e, sp_passed, full["xr"], G)
                load_adapters(G, 0, loraA, lambda b: GA[:, :, R * b:R * (b + 1)], ga_in)

            def load_lora_b(G):
                wait_alone(sp_e, sp_passed, full["cond"], K * G)
                load_adapters(G, 0, loraB, lambda b: GBA2[R * b:R * (b + 1), :], gb_in)

            def load_lora2(G):
                wait_alone(sp_e, sp_passed, full["A2T"], 2 * G)
                load_adapters(G, 1, lora2A, lambda b: GBA2[64 + R * b:64 + R * (b + 1), :], a2_in)
                wait_alone(sp_e, sp_passed, full["FB"], G)
                load_adapters(G, 1, lora2B, lambda b: B2g[:, :, R * b:R * (b + 1)], b2_in)

            def put_stack(g, i):
                t, par = K * g + i, i % 2
                for hl, made in enumerate([hi_made, taken["dtxT"]]):
                    wait_alone(sp_e, sp_passed, made, t + 1, stack_in[par], 32 * (K // 2 * g + i // 2))
                    sp_e.dma_start(parts_scratch[par, hl].rearrange("p a t -> a p t"),
                                   parts[:, hl, :].bitcast(fp32)).then_inc(parts_out, 16)
                wait_alone(sp_e, sp_passed, parts_out, 32 * (t + 1), dBx_full, UNITS * (t - 1))
                for hl in range(2):
                    sp_e.dma_start(
                        stack[64 * hl:64 * (hl + 1), par, :, :, :].bitcast(fp32).rearrange("p a tt d -> p (a tt d)"),
                        parts_scratch[par, hl].rearrange("p a t -> p (a t)").unsqueeze(0).to_broadcast([2, QT, P // QT * T]))\
                        .then_inc(stack_in[par], 16)

            def load_xres(G, j, t):
                wait(sp_e, x1_made, t - 1)
                sp_e.dma_start(xres[:, j % 2, :, :], of_group(x_tok, G)[:, :, P * j:P * (j + 1)])\
                    .then_inc(xres_in[j % 2], 16)

            def put_c(G):
                wait(sp_e, bc_made, 3 * G + 3)
                dst = c_scratch[G] if isinstance(G, int) else c_scratch[DynSlice(G, 1)].rearrange("o a c -> (o a) c")
                for hh in range(2):
                    for p in range(2):
                        sp_e.dma_start(
                            dst[2 * hh + p].rearrange("(b n t) -> n b t", b=2, n=HS),
                            BC[48 + HS * hh:48 + HS * (hh + 1), p * P:(p + 1) * P].rearrange("n (b t) -> n b t", b=2))\
                            .then_inc(cscr_out, 16)

            def spread_c(G, un):
                if un == 0:
                    wait(sp_e, cscr_out, 64 * G + 64)
                wait(sp_e, hC_made, UNITS * K * G - UNITS + un + 1)
                src = c_scratch[G] if isinstance(G, int) else c_scratch[DynSlice(G, 1)].rearrange("o a c -> (o a) c")
                sp_e.dma_start(Cb[:, un, :], src[un:un + 1, :].to_broadcast([P, UNIT])).then_inc(C_in[un], 16)

            def store(G, i):
                wait_alone(sp_e, sp_passed, taken["out"], 4 * G + i + 1)
                tt, half = i // 2, i % 2
                sp_e.dma_start(of_group(out_tok, G)[:, tt, half * 512:(half + 1) * 512], obuf[:, i % 2, :])\
                    .then_inc(out_done[i % 2], 16)

            sp_e.dma_start(idx[0:1, 0, :], ids1.rearrange("(o n) -> o n", o=1)).then_inc(s_idx, 16)
            sp_e.dma_start(idx[0:1, 1, :], ids2.rearrange("(o n) -> o n", o=1)).then_inc(s_idx, 16)
            for i in range(4):
                load_x(sp_e, 0, i)
            sp_e.dma_start(xproj_n, xproj_w).then_inc(s_setw, 16)
            sp_e.dma_start(dtproj_n, dtproj_w.rearrange("(k p) r -> p k r", p=P)).then_inc(s_setw, 16)
            sp_e.dma_start(negA[:, :, :], A_log.rearrange("(k p) n -> p k n", p=P)).then_inc(s_par, 16)
            sp_e.dma_start(dtprojT[DTR:DTR + 1, :], dtproj_b.rearrange("(o n) -> o n", o=1)).then_inc(s_par, 16)
            for dst, src in ((Dsb, Dw), (bias_sb, bias2)):
                sp_e.dma_start(dst[:, :], src.rearrange("(k p) -> p k", p=P),
                               allow_slow_non_contiguous=True).then_inc(s_par, 16)
            sp_e.dma_start(F_n[0:EM, :], expA.rearrange("e r d -> (e r) d")).then_inc(s_F, 16)
            sp_e.dma_start(F_n[EM:EM + E, :], router_w).then_inc(s_F, 16)
            for e in range(E):
                sp_e.dma_start(expB_n[:, :, R * e:R * (e + 1)], expB[e].rearrange("(k p) r -> p k r", p=P))\
                    .then_inc(s_F, 16)
            for half in range(2):
                sp_e.dma_start(Wsb[:, :, half * 512:(half + 1) * 512],
                               W.rearrange("(k p) o -> p k o", p=P)[:, :, half * 512:(half + 1) * 512]).then_inc((s_W0, s_W1)[half], 16)
                if half == 0:
                    sp_e.wait_ge(s_idx, 32)
                    load_lora_a(0)
                    load_lora_b(0)
            for k in range(K):
                wait(sp_e, gt_full, k - 3)
                sp_e.dma_start(W2c[k % 4], W2[P * k:P * (k + 1), :]).then_inc(s_W2[k % 4], 16)
                if k == 3:
                    put_c(0)
            put_stack(0, 0)
            for un in range(UNITS):
                spread_c(0, un)

            def body(G):
                last = isinstance(G, int) and G == GROUPS - 1
                first = isinstance(G, int) and G == 0
                for j in range(K):
                    t = K * G + j
                    for un in range(UNITS):
                        if un == 0:
                            if j:
                                load_xres(G, j - 1, t - 1)
                            elif not first:
                                load_xres(G - 1, K - 1, t - 1)
                        if (j, un) == (0, 0) and not last:
                            load_lora_a(G + 1)
                        if (j, un) == (0, 1):
                            if not first:
                                spread_c(G, UNITS - 1)
                            if not last:
                                load_lora_b(G + 1)
                        if (j, un) == (3, 2):
                            load_lora2(G)
                        if (j, un) == (6, 2) and not last:
                            put_c(G + 1)
                        for name, i, g in jobs_of(G, j, un):
                            if name == "dtxT":
                                put_stack(g, i)
                            if name == "out":
                                store(g, i)
                        if j == K - 1 and un >= 1 and not last:
                            spread_c(G + 1, un - 1)

            groups(sp_e, body)
            load_xres(GROUPS - 1, K - 1, K * GROUPS - 1)
            for i in range(4):
                store(GROUPS - 1, i)
            for s in out_done:
                sp_e.wait_ge(s, 16 * 2 * GROUPS)
            sp_e.wait_ge(cscr_out, 64 * GROUPS)

        @block.gpsimd
        def _(pool):
            made = 0

            def step(ins):
                nonlocal made
                made += 1
                ins.then_inc(s_cst, 1)
                pool.wait_ge(s_cst, made)

            def select(view, pattern, base, cm, op=ALU.not_equal, fill=1.0):
                step(pool.affine_select(out=view, in_=view, compare_op=op, fill=fill, base=base,
                                        pattern=pattern, channel_multiplier=cm))

            step(pool.memset(ident[:, :], 0.0))
            select(ident[:, :], [[-1, P]], 0, 1)
            step(pool.memset(own_batch[:, :], 1.0))
            v = own_batch[:, :].rearrange("p (b t) -> p b t", b=GB_)
            select(v, [[-R, GB_], [0, STEPS]], 0, 1, ALU.is_ge, 0.0)
            select(v, [[R, GB_], [0, STEPS]], R - 1, -1, ALU.is_ge, 0.0)
            step(pool.memset(own_rank[:, :, :], 0.0))
            for b in range(GB_):
                step(pool.memset(own_rank[STEPS * (b % 2):STEPS * (b % 2 + 1), b // 2, R * b:R * (b + 1)], 1.0))
            step(pool.memset(diag32[:, :], 0.0))
            for q in range(4):
                select(diag32[QT * q:QT * (q + 1), :], [[-1, QT]], 0, 1)
            step(pool.memset(before[:, :, :], 1.0))
            select(before[:, :, :], [[1, E], [-1, E]], 0, 0, ALU.is_gt, 0.0)
            for q in range(4):
                step(pool.memset(use_hi[QT * q:QT * (q + 1), :], float(q % 2 == 0)))
                step(pool.memset(use_lo[QT * q:QT * (q + 1), :], float(q % 2 == 1)))
            step(pool.memset(dtin[DTR:DTR + 1, :], 1.0))

            def make_dtx(t, i):
                pool.wait_ge(taken["dtz"], t + 1)
                wait(pool, full["dtxT"], t)
                pool.tensor_tensor(dtx[:, :], dt[:, i % NDT, :], u[:, i % K, :], ALU.mult).then_inc(dtx_made, 1)

            pool.wait_ge(taken["cond"], K)
            make_dtx(0, 0)
            make_dtx(1, 1)

            def body(G):
                for j in range(K):
                    for un in range(UNITS):
                        s = UNITS * (K * G + j) + un
                        pool.wait_ge(h_made, s + 1)
                        wait(pool, sum_done, s - NHC + 1)
                        if j == 0:
                            pool.wait_ge(C_in[un], 16 * G + 16)
                        pool.tensor_tensor(
                            hC[:, un % NHC, :].rearrange("p (n b t) -> p b n t", n=HS, b=2),
                            h[:, un % NH, :].rearrange("p (b n t) -> p b n t", n=HS, b=2),
                            Cb[:, un, :].rearrange("p (b n t) -> p b n t", n=HS, b=2), ALU.mult).then_inc(hC_made, 1)
                        for name, i, g in jobs_of(G, j, un - 1) if un else ():
                            if name == "dtz" and i != K:
                                make_dtx(K * g + i, i)
                        for name, i, g in jobs_of(G, j, un):
                            if (name, i) == ("dtz", K):
                                pool.wait_ge(taken["cond"], K * (g + 2))
                                make_dtx(K * g + i, i)

            groups(pool, body)

        @block.scalar
        def _(act):
            def softplus_parts(t, i, bank):
                act.wait_ge(full["dtz"], t + 1)
                wait(act, taken["dtz"], t)
                b = sp[:, :]
                act.activation(b, jb[bank][:, 0:T], ACT.Abs).then_inc(sp_step, 1)
                act.wait_ge(sp_step, 3 * t + 1)
                act.activation(b, b, ACT.Exp, scale=-1.0).then_inc(sp_step, 1)
                act.wait_ge(sp_step, 3 * t + 2)
                act.activation(b, b, ACT.Ln, bias=1.0).then_inc(sp_step, 1)
                wait(act, sum_done, UNITS * (t - 3))
                act.activation(Du[:, i % 4, :], u[:, i % K, :], ACT.Copy, scale=Dsb[:, i % K:i % K + 1]).then_inc(Du_made, 1)

            def decays(G, j, half, part):
                q = 2 * (K * G + j) + half
                if part == 0:
                    act.wait_ge(taken["dtz"], K * G + j + 1)
                    wait(act, h_made, 2 * (q - NDA) + 2)
                for n in range(4 * part, 4 * part + 4):
                    act.activation(
                        dA[:, half % NDA, :].rearrange("p (b n t) -> p b n t", b=GB_, n=HS)[:, :, n, 1:STEPS],
                        dt[:, j % NDT, :].rearrange("p (b t) -> p b t", b=GB_)[:, :, 1:STEPS],
                        ACT.Exp, scale=negA[:, j, HS * half + n:HS * half + n + 1]).then_inc(dA_made, 1)

            def job(name, i, g, bank):
                psum = jb[bank]
                if name == "dtz":
                    return softplus_parts(K * g + i, i, bank)
                if name in ("xr", "mid", "gate", "out"):
                    return
                if name == "mid2":
                    act.wait_ge(gate_step, GATE_STEPS * g + 2)
                    act.activation(gate[:, 1, :], gate[:, 0, :], ACT.Exp).then_inc(gate_exp, 1)
                    return
                act.wait_ge(full[name], nth(name, g, i))
                if name == "dtxT":
                    t = K * g + i
                    wait(act, parts_out, 32 * t)
                    act.activation(parts[:, 0, :], psum[:, 0:T], ACT.Copy).then_inc(hi_made, 1)
                elif name == "x1T":
                    act.activation(x1T[:, i % K, :], psum[:, 0:T], ACT.Copy).then_inc(taken[name], 1)
                elif name == "xT":
                    act.activation(xT[:, 2 * i:2 * i + 2, :].rearrange("p k t -> p (k t)"), psum[:, :], ACT.Copy)\
                        .then_inc(taken[name], 1)
                elif name == "cond":
                    wait(act, dtx_made, K * (g - 1) + i + 1)
                    wait(act, Du_made, K * (g - 1) + i + 1)
                    act.activation(u[:, i, :], psum[:, 0:T], ACT.Copy).then_inc(taken[name], 1)
                elif name == "xproj":
                    wait(act, cscr_out, 64 * g)
                    for s in out_done:
                        wait(act, s, 32 * (g - 1))
                    act.activation(dtin[0:DTR, :], psum[0:DTR, 0:T], ACT.Copy).then_inc(bc_made, 1)
                    act.activation(BC[DTR:2 * DTR, :], psum[DTR:2 * DTR, 0:T], ACT.Copy).then_inc(bc_made, 1)
                    act.activation(
                        B4[DTR:2 * DTR, :].rearrange("p (q a t) -> p q a t", q=NQ, a=4),
                        psum[DTR:2 * DTR, 0:T].rearrange("p (q t) -> p q t", q=NQ).unsqueeze(2)
                        .to_broadcast([DTR, NQ, 4, QT]), ACT.Copy).then_inc(bc_made, 1)
                elif name == "Bst":
                    act.activation(Bhl[:, 0, :], psum[:, 0:NQ * R], ACT.Copy).then_inc(b_step, 1)
                elif name == "A2T":
                    act.activation(G2[:, 4 * i:4 * i + 4, EM + E:], psum[:, 0:256].rearrange("p (k m) -> p k m", k=4),
                                   ACT.Copy).then_inc(taken[name], 1)
                elif name == "FB":
                    act.activation(FB[64:P, :], psum[64:P, 0:EM + E], ACT.Copy).then_inc(taken[name], 1)
                elif name == "h2T":
                    act.activation(low[64:P, :], psum[0:64, 0:T], ACT.Copy).then_inc(taken[name], 1)
                elif name == "gm":
                    act.activation(gm[:, :], psum[0:EM, 0:T], ACT.Copy).then_inc(taken[name], 1)

            act.add_instruction(mybir.InstLoadActFuncSet(name=nc.get_next_instruction_name(), act_func_set_id=LN_EXP_TABLES))
            act.wait_ge(s_par, 64)
            act.activation(negA[:, :, :], negA[:, :, :], ACT.Exp).then_inc(s_neg, 1)
            act.wait_ge(s_neg, 1)
            act.mul(negA[:, :, :], negA[:, :, :], -1.0).then_inc(s_neg, 1)
            act.wait_ge(s_neg, 2)
            act.wait_ge(s_cstv, 1)
            act.wait_ge(set_full, 1)
            act.activation(xprojT[:, :, :].rearrange("p k m -> p (k m)"), jb[0][:, :], ACT.Copy).then_inc(set_taken, 1)
            for i in range(2):
                act.wait_ge(set_full, 2 + i)
                act.activation(dtprojT[0:DTR, 512 * i:512 * (i + 1)], jb[1 - i][0:DTR, :], ACT.Copy).then_inc(set_taken, 1)
            for i in range(4):
                job("xT", i, 0, (i + 1) % 2)
            for i in range(2):
                act.wait_ge(set_full, 4 + i)
                act.activation(FT[:, 4 * i:4 * i + 4, :].rearrange("p k m -> p (k m)"), jb[1 - i][:, 0:4 * (EM + E)], ACT.Copy)\
                    .then_inc(set_taken, 1)
            for i in range(2):
                act.wait_ge(set_full, 6 + i)
                act.activation(expBT[:, 512 * i:512 * (i + 1)], jb[1 - i][0:EM, :], ACT.Copy).then_inc(set_taken, 1)
            for o in range(K):
                job("cond", o, 0, o % 2)
            job("xproj", 0, 0, 0)
            job("dtz", 0, 0, 1)
            job("Bst", 0, 0, 0)
            job("dtz", 1, 0, 1)
            job("dtxT", 0, 0, 0)
            decays(0, 0, 0, 0)
            decays(0, 0, 0, 1)
            act.wait_ge(gt_full, K)
            for i in range(2):
                act.activation(G_n[:, 512 * i:512 * (i + 1)], yp[i][0:EM + E, :], ACT.Copy).then_inc(gt_taken, 1)
            for i in range(2):
                act.wait_ge(set_full, 8 + i)
                act.activation(G2[:, 4 * i:4 * i + 4, 0:EM + E], jb[i][:, 0:4 * (EM + E)].rearrange("p (k m) -> p k m", k=4),
                               ACT.Copy).then_inc(set_taken, 1)
            act.wait_ge(set_full, 10)
            act.activation(cF[:, :], jb[0][:, 0:EM + E], ACT.Copy).then_inc(set_taken, 1)

            def body(G):
                last = isinstance(G, int) and G == GROUPS - 1
                if not last:
                    for i in range(4):
                        load_x(act, G + 1, i)
                for j in range(K):
                    for un in range(UNITS):
                        nj, nhalf = (j, 1) if un < 2 else (j + 1, 0)
                        if not (last and nj == K) and un in DECAYS_FIRST:
                            decays(G if nj < K else G + 1, nj % K, nhalf, un % 2)
                        for name, i, g in jobs_of(G, j, un):
                            job(name, i, g, BANK[name, i])
                        if not (last and nj == K) and un not in DECAYS_FIRST:
                            decays(G if nj < K else G + 1, nj % K, nhalf, un % 2)

            groups(act, body)
            job("x1T", K - 2, GROUPS - 1, 0)
            job("x1T", K - 1, GROUPS - 1, 1)
            job("h2T", 0, GROUPS - 1, 1)
            job("mid2", 0, GROUPS - 1, 0)
            job("gm", 0, GROUPS - 1, 1)

        @block.vector
        def _(dve):
            def step_size(t, i, bank):
                dve.wait_ge(sp_step, 3 * t + 3)
                wait(dve, dA_made, R * (t - NDT + 1))
                dve.scalar_tensor_tensor(dt[:, i % NDT, :], jb[bank][:, 0:T], 0.0, sp[:, :], ALU.max, ALU.add)\
                    .then_inc(taken["dtz"], 1)

            def add_residual(G, j, t):
                dve.wait_ge(sum_done, UNITS * (t + 1))
                dve.wait_ge(xres_in[j % 2], 16 * (K // 2 * G + j // 2 + 1))
                if j == 0:
                    wait(dve, taken["out"], 4 * G)
                dve.tensor_tensor(x1[:, :, P * j:P * (j + 1)], yp[j % 2][:, 0:T].rearrange("p (tt d) -> p tt d", tt=TT),
                                  xres[:, j % 2, :, :], ALU.add).then_inc(x1_made, 1)

            def b_diagonals(G, un):
                dve.wait_ge(b_step, 4 * G + 4)
                half, p = un // 2, un % 2
                of = [P, NQ // 2, HS, QT]
                dve.tensor_tensor(
                    Bd[:, NQ // 2 * p:NQ // 2 * (p + 1), HS * half:HS * (half + 1), :],
                    Bst[:, :].bitcast(fp32).rearrange("p (q n) -> p q n", q=NQ)
                    [:, NQ // 2 * p:NQ // 2 * (p + 1), HS * half:HS * (half + 1)].unsqueeze(3).to_broadcast(of),
                    diag32[:, :].unsqueeze(1).unsqueeze(1).to_broadcast(of), ALU.mult).then_inc(Bd_made, 1)

            def te(i):
                return gate[:, i, :].rearrange("p (a e) -> p a e", a=TT)

            def ee(i):
                return beats[:, i, :].rearrange("p (a e f) -> p (a e) f", e=E, f=E)

            def gating(g, second):
                n = 6 if second else 0

                def link(ins):
                    nonlocal n
                    n += 1
                    ins.then_inc(gate_step, 1)
                    dve.wait_ge(gate_step, GATE_STEPS * g + n)

                shape = [P, TT, E]
                if not second:
                    logits = mids[:, :, EM:EM + E]
                    top = gate[:, 2, 0:TT]
                    link(dve.tensor_reduce(top, logits, AX.X, ALU.max))
                    link(dve.tensor_tensor(te(0), logits, top.unsqueeze(2).to_broadcast(shape), ALU.subtract))
                    for tt in range(TT):
                        other = logits[:, tt, :].unsqueeze(1).to_broadcast([P, E, E])
                        own = logits[:, tt, :].unsqueeze(2).to_broadcast([P, E, E])
                        dve.tensor_tensor(ee(0)[:, E * tt:E * (tt + 1), :], other, own, ALU.is_gt)
                        last = dve.tensor_tensor(ee(1)[:, E * tt:E * (tt + 1), :], other, own, ALU.is_equal)
                    link(last)
                    for tt in range(TT):
                        last = dve.tensor_tensor(ee(1)[:, E * tt:E * (tt + 1), :], ee(1)[:, E * tt:E * (tt + 1), :],
                                                 before[:, :, :], ALU.mult)
                    link(last)
                    link(dve.tensor_tensor(beats[:, 0, :], beats[:, 0, :], beats[:, 1, :], ALU.add))
                    link(dve.tensor_reduce(gate[:, 3, :], ee(0), AX.X, ALU.add))
                    assert n == 6
                    return
                dve.wait_ge(gate_exp, g + 1)
                link(dve.scalar_tensor_tensor(gate[:, 1, :], gate[:, 3, :], 1.5, gate[:, 1, :], ALU.is_lt, ALU.mult))
                link(dve.tensor_reduce(gate[:, 2, 0:TT], te(1), AX.X, ALU.add))
                link(dve.reciprocal(gate[:, 3, 0:TT], gate[:, 2, 0:TT]))
                link(dve.scalar_tensor_tensor(te(4), te(1), LORA2_SCALE, gate[:, 3, 0:TT].unsqueeze(2).to_broadcast(shape),
                                              ALU.mult, ALU.mult))
                assert n == GATE_STEPS
                for tt in range(TT):
                    last = dve.tensor_tensor(
                        gmT[:, tt, :].rearrange("p (e r) -> p e r", e=E),
                        mids[:, tt, 0:EM].rearrange("p (e r) -> p e r", e=E),
                        te(4)[:, tt, :].unsqueeze(2).to_broadcast([P, E, R]), ALU.mult)
                last.then_inc(gated, 1)

            def job(name, i, g, bank):
                if name == "gate":
                    return gating(g, True)
                psum = jb[bank]
                if name == "dtz":
                    return step_size(K * g + i, i, bank)
                if name == "dtxT":
                    t = K * g + i
                    dve.wait_ge(hi_made, t + 1)
                    dve.tensor_tensor(parts[:, 1, :], psum[:, 0:T], parts[:, 0, :].bitcast(fp32), ALU.subtract)\
                        .then_inc(taken[name], 1)
                elif name == "xr":
                    dve.wait_ge(full[name], g + 1)
                    dve.tensor_tensor(low[0:64, :], psum[0:64, 0:T], own_batch[0:64, :], ALU.mult).then_inc(taken[name], 1)
                elif name == "Bst":
                    dve.wait_ge(b_step, 4 * g + 1)
                    dve.tensor_tensor(Bhl[:, 1, :], psum[:, 0:NQ * R], Bhl[:, 0, :].bitcast(fp32), ALU.subtract)\
                        .then_inc(b_step, 1)
                    dve.wait_ge(b_step, 4 * g + 2)
                    dve.tensor_scalar(Bst[:, :], Bhl[:, 0, :].bitcast(fp32), use_hi[:, :], None, ALU.mult).then_inc(b_step, 1)
                    dve.wait_ge(b_step, 4 * g + 3)
                    dve.scalar_tensor_tensor(Bst[:, :], Bhl[:, 1, :].bitcast(fp32), use_lo[:, :], Bst[:, :].bitcast(fp32),
                                             ALU.mult, ALU.add).then_inc(b_step, 1)
                elif name == "mid":
                    dve.wait_ge(h2_raw, g + 1)
                    dve.tensor_tensor(h2m[:, :, :], psum[:, 0:TT * G2W].rearrange("p (a c) -> p a c", a=TT)[:, :, EM + E:],
                                      own_rank[:, :, :], ALU.mult).then_inc(h2_masked, 1)
                elif name == "mid2":
                    dve.wait_ge(full["mid"], g + 1)
                    dve.tensor_tensor(mids[:, :, :], psum[:, 0:TT * G2W].rearrange("p (a c) -> p a c", a=TT)[:, :, 0:EM + E],
                                      cF[:, :].unsqueeze(1).to_broadcast([P, TT, EM + E]), ALU.add).then_inc(taken["mid"], 1)
                    dve.wait_ge(taken["mid"], g + 1)
                    gating(g, False)
                elif name == "out":
                    dve.wait_ge(full[name], 4 * g + i + 1)
                    if i >= 2:
                        wait(dve, out_done[i % 2], 16 * (2 * g + 1))
                    tt, half = i // 2, i % 2
                    dve.tensor_tensor(obuf[:, i % 2, :], psum[:, :], x1[:, tt, half * 512:(half + 1) * 512], ALU.add)\
                        .then_inc(taken[name], 1)

            for i in range(NDA):
                last = dve.memset(dA[:, i, :].rearrange("p (b n t) -> p (b n) t", b=GB_, n=HS)[:, :, 0:1], 0.0)
            last.then_inc(s_cstv, 1)
            dve.wait_ge(s_cst, CONSTS)
            job("xr", 0, 0, 1)
            job("dtz", 0, 0, 1)
            job("Bst", 0, 0, 0)
            for un in range(UNITS):
                b_diagonals(0, un)
            job("dtz", 1, 0, 1)
            job("dtxT", 0, 0, 0)

            def body(G):
                first, final = (isinstance(G, int) and G == g for g in (0, GROUPS - 1))
                for j in range(K):
                    t = K * G + j
                    for un in range(UNITS):
                        s, half, p = UNITS * t + un, un // 2, un % 2
                        if un == UNITS - 1 and j == 0 and not first:
                            add_residual(G - 1, K - 1, t - 1)
                        if un == UNITS - 1 and j == 2:
                            add_residual(G, 0, t - 2)
                        if un == UNITS - 1 and j >= 2:
                            add_residual(G, j - 1, t - 1)
                        dve.wait_ge(dBx_full, s + 1)
                        dve.wait_ge(dA_made, R * t + HS * (half + 1))
                        wait(dve, hC_made, s - NH + 1)
                        dve.tensor_tensor_scan(h[:, un % NH, :], dA[:, half % NDA, UNIT * p:UNIT * (p + 1)], dBx[un % 2][:, :],
                                               0.0, ALU.mult, ALU.add).then_inc(h_made, 1)
                        if j == K - 1 and not final:
                            b_diagonals(G + 1, un)
                        for name, i, g in jobs_of(G, j, un - 1) if un else ():
                            if (name, i) in LATE:
                                job(name, i, g, BANK[name, i])
                        for name, i, g in jobs_of(G, j, un):
                            if (name, i) not in LATE:
                                job(name, i, g, BANK[name, i])

            groups(dve, body)
            add_residual(GROUPS - 1, K - 1, K * GROUPS - 1)
            job("mid", 0, GROUPS - 1, 0)
            job("mid2", 0, GROUPS - 1, 0)
            job("gate", 0, GROUPS - 1, 0)
            for i in range(4):
                job("out", i, GROUPS - 1, i % 2)

        @block.tensor
        def _(pe):
            tenant = {}

            def mm(o, lhsT, rhs, start, stop, **kw):
                return pe.matmul(o, lhsT, rhs, start=start, stop=stop, **kw)

            def tr(o, in_, n, first=0):
                return pe.matmul(o, in_, ident[first:first + n, first:first + n], is_transpose=True, start=True, stop=True)

            def job(name, i, g, bank):
                operand = {"Bst": (bc_made, 3 * g + 3), "A2T": (a2_in, 64 * g + 64),
                           "h2T": (h2_masked, g + 1), "gm": (gated, g + 1)}.get(name, ())
                if name == "gate":
                    return
                if name == "mid2":
                    psum = jb[bank]
                    pe.wait_ge(taken["h2T"], g + 1)
                    pe.wait_ge(taken["FB"], g + 1)
                    for tt in range(TT):
                        last = mm(psum[:, G2W * tt:G2W * tt + EM + E], low[64:P, P * tt:P * (tt + 1)], FB[64:P, :],
                                  False, True, skip_group_check=True)
                    last.then_inc(full["mid"], 1)
                    return
                if operand:
                    wait_alone(pe, pe_passed, *tenant.get(bank, ()), *operand)
                elif bank in tenant:
                    wait(pe, *tenant[bank])
                tenant[bank] = (taken[name], nth(name, g, i))
                psum = jb[bank]
                if name == "dtz":
                    pe.wait_ge(bc_made, 3 * (g if i < K else g + 1) + 1)
                    last = mm(psum[:, 0:T], dtprojT[:, P * (i % K):P * (i % K + 1)], dtin[:, :], True, True)
                elif name == "dtxT":
                    pe.wait_ge(dtx_made, K * g + i + 1)
                    for tt in range(TT):
                        last = tr(psum[:, P * tt:P * (tt + 1)], dtx[:, P * tt:P * (tt + 1)], P)
                elif name == "x1T":
                    pe.wait_ge(x1_made, K * g + i + 1)
                    for tt in range(TT):
                        last = tr(psum[:, P * tt:P * (tt + 1)], x1[:, tt, P * (i % K):P * (i % K + 1)], P)
                elif name == "xT":
                    pe.wait_ge(xin_in[i], 16 * (g + 1))
                    for a in range(2):
                        for tt in range(TT):
                            c = (a * TT + tt) * P
                            last = tr(psum[:, c:c + P], xin[:, i, tt, P * a:P * (a + 1)], P)
                elif name == "xr":
                    pe.wait_ge(taken["xT"], 4 * g + 4)
                    pe.wait_ge(ga_in, 64 * g + 64)
                    for k in range(K):
                        last = mm(psum[0:64, 0:T], GA[:, k, :], xT[:, k, :], k == 0, k == K - 1)
                elif name == "cond":
                    for k in range(K):
                        mm(psum[:, 0:T], Wsb[:, k, P * i:P * (i + 1)], xT[:, k, :], k == 0, False)
                    if i == 0:
                        pe.wait_ge(taken["xr"], g + 1)
                        pe.wait_ge(gb_in, 64 * g + 64)
                    last = mm(psum[:, 0:T], GBA2[0:64, P * i:P * (i + 1)], low[0:64, :], False, True)
                elif name == "xproj":
                    pe.wait_ge(taken["cond"], K * g + K)
                    for k in range(K):
                        last = mm(psum[0:2 * DTR, 0:T], xprojT[:, k, :], u[:, k, :], k == 0, k == K - 1)
                    tenant[bank] = (bc_made, 3 * g + 3)
                elif name == "Bst":
                    for q in range(NQ):
                        last = pe.matmul(psum[:, R * q:R * (q + 1)], B4[DTR:DTR + R, P * q:P * (q + 1)],
                                         ident[DTR:DTR + R, DTR:DTR + R], is_transpose=True, start=True, stop=True)
                    tenant[bank] = (b_step, 4 * g + 2)
                elif name == "A2T":
                    for a in range(4):
                        k = 4 * i + a
                        last = tr(psum[:, 64 * a:64 * (a + 1)], GBA2[64:P, P * k:P * (k + 1)], 64, 64)
                elif name == "FB":
                    pe.wait_ge(b2_in, 64 * g + 64)
                    for k in range(K):
                        last = mm(psum[64:P, 0:EM + E], B2g[:, k, :], FT[:, k, :], k == 0, k == K - 1)
                elif name == "mid":
                    pe.wait_ge(taken["x1T"], K * g + K)
                    pe.wait_ge(taken["A2T"], 2 * g + 2)
                    for tt in range(TT):
                        for k in range(K):
                            last = mm(psum[:, G2W * tt:G2W * (tt + 1)], x1T[:, k, P * tt:P * (tt + 1)], G2[:, k, :],
                                      k == 0 and tt == 0, False, skip_group_check=True)
                    last.then_inc(h2_raw, 1)
                    return
                elif name == "h2T":
                    for tt in range(TT):
                        last = tr(psum[0:64, P * tt:P * (tt + 1)], h2m[:, tt, :], P)
                elif name == "gm":
                    for tt in range(TT):
                        last = tr(psum[0:EM, P * tt:P * (tt + 1)], gmT[:, tt, :], P)
                elif name == "out":
                    pe.wait_ge(taken["gm"], g + 1)
                    tt, half = i // 2, i % 2
                    last = mm(psum[:, :], gm[:, P * tt:P * (tt + 1)], expBT[:, half * 512:(half + 1) * 512], True, True)
                last.then_inc(full[name], 1)

            def b_times_dtx(G, j, un):
                t = K * G + j
                s, half, p = UNITS * t + un, un // 2, un % 2
                if un == 0:
                    pe.wait_ge(stack_in[j % 2], 32 * (K // 2 * G + j // 2 + 1))
                if j == 0:
                    pe.wait_ge(Bd_made, UNITS * G + un + 1)
                wait(pe, h_made, s - 1)
                for b in range(2):
                    for a in range(2):
                        q = 4 * p + 2 * b + a
                        o = dBx[un % 2][:, 512 * b:512 * (b + 1)].rearrange("p (n t) -> p n t", n=HS)[:, :, QT * a:QT * (a + 1)]
                        last = mm(o, stack[:, j % 2, q % 4, q // 4, :],
                                  Bd[:, q, HS * half:HS * (half + 1), :].rearrange("p n t -> p (n t)"),
                                  True, True, skip_group_check=True)
                last.then_inc(dBx_full, 1)

            def sum_states(G, j, un):
                t = K * G + j
                half, p = un // 2, un % 2
                pe.wait_ge(hC_made, UNITS * t + un + 1)
                if un == 0:
                    wait(pe, x1_made, t - 1)
                y = yp[j % 2][:, P * p:P * (p + 1)]
                for n in range(HS):
                    last = pe.matmul(y, hC[:, un % NHC, P * n:P * (n + 1)], ident[:, :], is_transpose=True,
                                     start=un == 0 and n == 0, stop=False, skip_group_check=True)
                if half == 1:
                    if p == 0:
                        pe.wait_ge(Du_made, t + 1)
                    last = pe.matmul(y, Du[:, j % 4, P * p:P * (p + 1)], ident[:, :], is_transpose=True,
                                     start=False, stop=True, skip_group_check=True)
                last.then_inc(sum_done, 1)

            def set_up(bank, n):
                wait(pe, set_taken, n)

            pe.wait_ge(s_cst, CONSTS)
            pe.wait_ge(s_setw, 32)
            for k in range(K):
                last = tr(jb[0][:, 64 * k:64 * (k + 1)], xproj_n[:, P * k:P * (k + 1)], 64)
            last.then_inc(set_full, 1)
            for i in range(2):
                set_up(1 - i, i)
                for a in range(4):
                    last = tr(jb[1 - i][0:DTR, P * a:P * (a + 1)], dtproj_n[:, 4 * i + a, :], P)
                last.then_inc(set_full, 1)
            tenant[1], tenant[0] = (set_taken, 2), (set_taken, 3)
            for i in range(4):
                job("xT", i, 0, (i + 1) % 2)
            pe.wait_ge(s_F, 96)
            n = EM + E
            for i in range(2):
                wait(pe, taken["xT"], 3 + i)
                for a in range(4):
                    last = tr(jb[1 - i][:, n * a:n * (a + 1)], F_n[:, P * (4 * i + a):P * (4 * i + a + 1)], n)
                last.then_inc(set_full, 1)
            for i in range(2):
                set_up(1 - i, 4 + i)
                for a in range(4):
                    last = tr(jb[1 - i][0:EM, P * a:P * (a + 1)], expB_n[:, 4 * i + a, :], P)
                last.then_inc(set_full, 1)
            tenant[1], tenant[0] = (set_taken, 6), (set_taken, 7)
            job("xr", 0, 0, 1)
            pe.wait_ge(s_W0, 16)
            for o in range(K):
                if o == 4:
                    pe.wait_ge(s_W1, 16)
                job("cond", o, 0, o % 2)
            pe.wait_ge(s_par, 64)
            job("xproj", 0, 0, 0)

            def times_W2(k):
                pe.wait_ge(s_W2[k % 4], 16 * (k // 4 + 1))
                for c in range(2):
                    last = mm(yp[c][0:n, :], FT[:, k, :], W2c[k % 4][:, 512 * c:512 * (c + 1)], k == 0, k == K - 1)
                last.then_inc(gt_full, 1)

            times_W2(0)
            job("dtz", 0, 0, 1)
            times_W2(1)
            job("Bst", 0, 0, 0)
            times_W2(2)
            job("dtz", 1, 0, 1)
            times_W2(3)
            job("dtxT", 0, 0, 0)
            for k in range(4, K):
                times_W2(k)
            wait_alone(pe, pe_passed, gt_taken, 2, taken["dtz"], 2, taken["dtxT"], 1)
            for i in range(2):
                for a in range(4):
                    last = tr(jb[i][:, n * a:n * (a + 1)], G_n[:, P * (4 * i + a):P * (4 * i + a + 1)], n)
                last.then_inc(set_full, 1)
            wait(pe, set_taken, 8)
            for k in range(K):
                last = mm(jb[0][:, 0:n], bias_sb[:, k:k + 1].to_broadcast([P, P]), FT[:, k, :], k == 0, k == K - 1)
            last.then_inc(set_full, 1)
            pe.wait_ge(set_taken, 10)

            def body(G):
                first = isinstance(G, int) and G == 0
                tenant.clear()
                if not first:
                    for bank, (name, i) in LAST_JOB.items():
                        tenant[bank] = (taken[name], nth(name, G - 1, i))
                for j in range(K):
                    for un in range(UNITS):
                        b_times_dtx(G, j, un)
                        back = UNITS * j + un - LAG
                        if back >= 0:
                            sum_states(G, back // UNITS, back % UNITS)
                        elif not first:
                            sum_states(G - 1, K - 1, back % UNITS)
                        for name, i, g in jobs_of(G, j, un):
                            job(name, i, g, BANK[name, i])

            groups(pe, body)
            G = GROUPS - 1
            for un in range(UNITS - LAG, UNITS):
                sum_states(G, K - 1, un)
            job("x1T", K - 2, G, 0)
            job("x1T", K - 1, G, 1)
            job("mid", 0, G, 0)
            job("h2T", 0, G, 1)
            job("mid2", 0, G, 0)
            job("gm", 0, G, 1)
            for i in range(4):
                job("out", i, G, i % 2)


LN_EXP_TABLES = 6
GATE_STEPS = 10
DECAYS_FIRST = (1, 2, 3)
G2W = EM + E + GB_ * R
CONSTS = 26

_INS = ['x', 'itok_B_0_15', 'itok_B_6_15', 'L0_cond_W', 'L0_cond_lora_A', 'L0_cond_lora_B', 'L0_attn_A_log', 'L0_attn_D',
        'L0_attn_x_proj_w', 'L0_attn_dt_proj_w', 'L0_attn_dt_proj_b', 'L0_cond2_base_weight', 'L0_cond2_base_bias',
        'L0_cond2_lora_A_w', 'L0_cond2_lora_B_w', 'L0_ffn_router_w', 'L0_ffn_A', 'L0_ffn_B']


def kernel(**inputs):
    import numpy as _np
    import concourse.bacc as _bacc
    from concourse import mybir as _mybir
    from concourse.bass_utils import run_bass_kernel_spmd as _run

    nc = _bacc.Bacc("TRN2", target_bir_lowering=False, num_devices=1)
    arrays, args = {}, []
    for name in _INS:
        a = _np.ascontiguousarray(inputs[name])
        arrays[f"in_{name}"] = a
        args.append(nc.dram_tensor(f"in_{name}", a.shape, _mybir.dt.from_np(a.dtype), kind="ExternalInput").ap())
    o = nc.dram_tensor("out_0", (BATCHES, STEPS, D), _mybir.dt.float32, kind="ExternalOutput").ap()
    layer_kernel(nc, *args, o)
    r = _run(nc, [arrays], core_ids=[0])
    return r.results[0]["out_0"]
```

```python
import concourse.bass as bass
from concourse import mybir
from contextlib import ExitStack

P = 128
BATCHES, STEPS, D = 32, 64, 1024
R = 16
GROUPS = 8
GB_ = BATCHES // GROUPS
T = GB_ * STEPS
TT = T // P
K = D // P
DTR = 32
E = 4
EM = E * R
HS = R // 2
UNIT = HS * P
UNITS = 4
QT = 32
NQ = T // QT
LAG = 3
NDA, NH, NHC, NDT = 2, 2, 4, 4
PARTS = ((0, 0), (0, 1), (1, 0))
LORA2_SCALE = 16.0 / 16.0 ** 0.5

JOBS = {
    (0, 0): [("x1T", -2), ("dtxT", 1), ("dtz", 2)],
    (0, 1): [("xT", 0), ("xT", 1)],
    (0, 2): [("xT", 2), ("xT", 3)],
    (0, 3): [("GAs", 0), ("x1T", -1), ("xr", 0)],
    (1, 0): [("dtxT", 2), ("dtz", 3), ("mid", 0)],
    (1, 2): [("h2T", 0), ("mid2", 0)],
    (1, 3): [("cond", 0), ("gate", 0)],
    (2, 0): [("dtxT", 3), ("dtz", 4), ("gm", 0)],
    (2, 1): [("out", 0), ("out", 1)],
    (2, 2): [("out", 2), ("out", 3), ("cond", 1)],
    (3, 0): [("x1T", 0), ("x1T", 1), ("dtxT", 4), ("dtz", 5)],
    (3, 1): [("cond", 2)],
    (3, 3): [("cond", 3)],
    (4, 0): [("x1T", 2), ("dtxT", 5), ("dtz", 6)],
    (4, 1): [("cond", 4)],
    (4, 3): [("cond", 5)],
    (5, 0): [("x1T", 3), ("dtxT", 6), ("dtz", 7)],
    (5, 1): [("cond", 6)],
    (5, 3): [("cond", 7), ("dtxT", 7)],
    (6, 0): [("x1T", 4)],
    (6, 1): [("xproj", 0)],
    (6, 2): [("dtz", 8), ("Bst", 0)],
    (7, 0): [("x1T", 5), ("dtz", 9), ("dtxT", 8)],
    (7, 2): [("A2T", 0), ("A2T", 1)],
    (7, 3): [("FB", 0)],
}
LATE = {("Bst", 0), ("dtz", 0), ("dtz", 1), ("dtz", 2), ("dtz", 3), ("dtz", 4), ("dtz", 5), ("dtz", 6), ("dtz", 7), ("dtz", 8), ("dtz", 9)}
BANK, LAST_JOB = {}, {}
_b = 1
for _at in sorted(JOBS):
    for _job in JOBS[_at]:
        if _job[0] == "GAs":
            BANK[_job] = None
        elif _job[0] not in ("mid2", "gate"):
            _b = 1 - BANK["mid", 0] if ("mid", 0) in BANK and ("mid2", 0) not in BANK else 1 - _b
            BANK[_job], LAST_JOB[_b] = _b, _job
        else:
            BANK[_job], _b = BANK["mid", 0], BANK["mid", 0]
OF_PREVIOUS = {"mid", "h2T", "mid2", "gate", "gm", "out"}
OF_NEXT = {"xT", "GAs", "xr", "cond", "xproj", "Bst"}


def layer_kernel(nc, x, ids1, ids2, W, loraA, loraB, A_log, Dw, xproj_w, dtproj_w, dtproj_b,
                 W2, bias2, lora2A, lora2B, router_w, expA, expB, out):
    fp32, fr, i32 = mybir.dt.float32, mybir.dt.float32r, mybir.dt.int32
    ALU, ACT, AX = mybir.AluOpType, mybir.ActivationFunctionType, mybir.AxisListType
    DynSlice = bass.DynSlice

    ctx = ExitStack()
    with ctx:
        def sb(name, shape, dt=fp32):
            return ctx.enter_context(nc.sbuf_tensor(name, shape, dt))

        def sem(name):
            return ctx.enter_context(nc.semaphore(name))

        ident = sb("ident", [P, P])
        diag32 = sb("diag32", [P, QT])
        own_batch = sb("own_batch", [GB_ * R, T])
        own_rank = sb("own_rank", [P, TT, GB_ * R])
        use_hi = sb("use_hi", [P, 1])
        use_lo = sb("use_lo", [P, 1])
        before = sb("before", [P, E, E])
        idx = sb("idx", [1, 2, BATCHES], i32)
        negA = sb("negA", [P, K, R])
        Dsb = sb("Dsb", [P, K])
        xprojT = sb("xprojT", [P, K, 2 * DTR])
        dtprojT = sb("dtprojT", [3 * DTR + 2, D], fr)
        FT = sb("FT", [P, K, EM + E])
        G2 = sb("G2", [P, K, EM + E + GB_ * R])
        cF = sb("cF", [P, EM + E])
        bias_sb = sb("bias_sb", [P, K])
        expBT = sb("expBT", [EM, D])

        xin = sb("xin", [P, 4, TT, 2 * P])
        Wst = sb("Wst", [P, 2, 2, K, P], fr)
        xT = sb("xT", [P, 2, K, T], fr)
        GA = sb("GA", [P, K, GB_ * R])
        GAs = sb("GAs", [P, 2, K, GB_ * R], fr)
        GBA2 = sb("GBA2", [P, D])
        B2g = sb("B2g", [P, K, GB_ * R])
        FB = sb("FB", [P, EM + E])
        low = sb("low", [P, T])
        u = sb("u", [P, K, T])
        dtin = sb("dtin", [3 * DTR + 2, T], fr)
        BC = sb("BC", [2 * DTR, T])
        Bhl = sb("Bhl", [P, 2, NQ * R], fr)
        Bst = sb("Bst", [P, NQ * R], fr)
        Bd = sb("Bd", [P, NQ, R, QT], fr)
        Cb = sb("Cb", [P, UNITS, UNIT])
        x1 = sb("x1", [P, TT, D])
        x1T = sb("x1T", [P, K, T])
        h2m = sb("h2m", [P, TT, GB_ * R])
        mids = sb("mids", [P, TT, EM + E])
        gmT = sb("gmT", [P, TT, EM])
        gm = sb("gm", [EM, T])
        obuf = sb("obuf", [P, 2, D // 2])
        beats = sb("beats", [P, 2, TT * E * E])
        gate = sb("gate", [P, 6, TT * E])
        B4 = obuf[:, :, :].rearrange("p a c -> p (a c)")

        sp = sb("sp", [P, T])
        dt = sb("dt", [P, NDT, T])
        dtx = sb("dtx", [P, T])
        Du = sb("Du", [P, 4, T])
        parts = sb("parts", [P, 2, T], fr)
        stack = sb("stack", [P, 2, P // QT, TT, P], fr)
        dA = sb("dA", [P, NDA, GB_ * HS * STEPS])
        h = sb("h", [P, NH, UNIT])
        hC = sb("hC", [P, NHC, UNIT])
        xres = sb("xres", [P, 2, TT, P])

        W2c = [x1T[:, 0:4, :].rearrange("p k t -> p (k t)"), x1T[:, 4:8, :].rearrange("p k t -> p (k t)"),
               x1[:, 0, :], x1[:, 1, :]]
        Wraw = [Cb[:, :, :].rearrange("p u c -> p (u c)").rearrange("p (k o) -> p k o", k=K // 2),
                dA[:, :, :].rearrange("p h c -> p (h c)").rearrange("p (k o) -> p k o", k=K // 2)]
        b_raw = h[0:1, 0, :]
        b_part = [stack[0:1, i, :, :, :].rearrange("p a tt d -> p (a tt d)") for i in range(2)]
        G_n = h[0:EM + E, 1, :]
        hCf = hC[:, :, :].rearrange("p a c -> p (a c)")
        xproj_n = hCf[0:2 * DTR, 0:D]
        F_n = hCf[0:EM + E, D:2 * D]
        expB_n = hCf[:, 2 * D:2 * D + K * EM].rearrange("p (k m) -> p k m", k=K)
        dtproj_n = hCf[:, 2 * D + K * EM:2 * D + K * EM + K * DTR].rearrange("p (k m) -> p k m", k=K)

        dBx = [ctx.enter_context(nc.psum_tensor(f"dBx{i}", [P, UNIT], fp32)) for i in range(2)]
        yp = [ctx.enter_context(nc.psum_tensor(f"yp{i}", [P, 512], fp32)) for i in range(2)]
        jb = [ctx.enter_context(nc.psum_tensor(f"jb{i}", [P, 512], fp32)) for i in range(2)]

        parts_scratch = nc.dram_tensor("parts_scratch", [2, 2, QT, P // QT, T], fp32, kind="Internal").ap()
        W_scratch = nc.dram_tensor("W_scratch", [K, P, 2 * K * P], fp32, kind="Internal").ap()
        c_scratch = nc.dram_tensor("c_scratch", [GROUPS, UNITS, UNIT], fp32, kind="Internal").ap()

        s_idx, s_W0, s_W1, s_par, s_setw, s_F = map(sem, ["idx_in", "W0_in", "W1_in", "params_in", "proj_in", "F_in"])
        s_W2 = [sem(f"W2c{i}_in") for i in range(4)]
        xin_in = [sem(f"xin{i}_in") for i in range(4)]
        ga_in, gb_in, a2_in, b2_in = map(sem, ["ga_in", "gb_in", "a2_in", "b2_in"])
        stack_in = [sem("stack0_in"), sem("stack1_in")]
        xres_in = [sem("xres0_in"), sem("xres1_in")]
        parts_out = sem("parts_out")
        Wh_made, Wl_made, xh_made, GAh_made, GA_split = map(sem, ["Wh_made", "Wl_made", "xh_made", "GAh_made", "GA_split"])
        W_out = [sem("W_scratch0_out"), sem("W_scratch1_out")]
        W_in = [sem("Wst0_in"), sem("Wst1_in")]
        s_bias, b_split, w_hi, dtin_hi, dtin_lo = map(sem, ["bias_in", "bias_split", "w_hi", "dtin_hi", "dtin_lo"])
        cscr_out = sem("c_scratch_out")
        C_in = [sem(f"C{i}_in") for i in range(UNITS)]
        out_done = [sem("out0_done"), sem("out1_done")]
        s_cst, s_cstv, s_neg = map(sem, ["consts_made", "consts_made_dve", "negA_made"])
        set_full, set_taken, gt_full, gt_taken = map(sem, ["setup_full", "setup_taken", "gt_full", "gt_taken"])
        full, taken = {}, {}
        for _n in ["dtz", "x1T", "dtxT", "xT", "xr", "cond", "mid", "h2T", "gm", "out", "xproj", "Bst", "A2T", "FB"]:
            full[_n], taken[_n] = sem(_n + "_full"), sem(_n + "_taken")
        per_group = {"dtz": K, "x1T": K, "dtxT": K, "xT": 4, "cond": K, "out": 4, "A2T": 2}
        h2_raw, h2_masked, gated = sem("h2_raw"), sem("h2_masked"), sem("gated")
        sp_step, dtx_made, Du_made, hi_made = map(sem, ["softplus_step", "dtx_made", "Du_made", "hi_made"])
        bc_made, b_step, Bd_made = map(sem, ["bc_made", "b_step", "Bd_made"])
        gate_step, gate_exp = sem("gate_step"), sem("gate_exp")
        dA_made, dBx_full, h_made, hC_made, sum_done, x1_made = map(
            sem, ["dA_made", "dBx_full", "h_made", "hC_made", "sum_done", "x1_made"])

        pe_passed, sp_passed = sem("pe_passed"), sem("sp_passed")

        block = ctx.enter_context(nc.Block())

        def wait(eng, s, value):
            if not isinstance(value, int) or value > 0:
                eng.wait_ge(s, value)

        def wait_alone(eng, passed, *waits):
            for s, v in zip(waits[::2], waits[1::2]):
                wait(eng, s, v)
                eng.sem_inc(passed, 1)

        def nth(name, G, i):
            return per_group.get(name, 1) * G + i + 1

        def group_of(name, G):
            return G - 1 if name in OF_PREVIOUS else G + 1 if name in OF_NEXT else G

        def jobs_of(G, j, un):
            first, last = isinstance(G, int) and G == 0, isinstance(G, int) and G == GROUPS - 1
            for name, i in JOBS.get((j, un), ()):
                if first and (name in OF_PREVIOUS or (name == "x1T" and i < 0)):
                    continue
                if last and (name in OF_NEXT or (name in ("dtz", "dtxT") and i >= K)):
                    continue
                yield name, i, group_of(name, G)

        def groups(eng, body):
            body(0)
            with eng.Fori(1, GROUPS - 1) as G:
                body(G)
            body(GROUPS - 1)

        x_tok = x.rearrange("b s d -> (b s) d").rearrange("(g tt p) d -> g p tt d", tt=TT, p=P)
        out_tok = out.rearrange("b s d -> (b s) d").rearrange("(g tt p) d -> g p tt d", tt=TT, p=P)

        def of_group(ap, G):
            return ap[G] if isinstance(G, int) else ap[DynSlice(G, 1)].rearrange("o p tt d -> (o p) tt d")

        def load_x(eng, G, i):
            wait(eng, taken["xT"], 4 * (G - 1) + i + 1)
            eng.dma_start(xin[:, i, :, :], of_group(x_tok, G)[:, :, 2 * P * i:2 * P * (i + 1)]).then_inc(xin_in[i], 16)

        @block.sync
        def _(sp_e):

            def load_adapters(G, which, table, dst, s):
                for b in range(GB_):
                    v = sp_e.value_load(idx[0:1, which, DynSlice(G * GB_ + b, 1)], min_val=0, max_val=table.shape[0] - 1)
                    sp_e.dma_start(dst(b), table[DynSlice(v, 1)].rearrange(
                        "o (k p) r -> p (o k) r" if table.shape[1] == D else "o r d -> (o r) d",
                        **({"p": P} if table.shape[1] == D else {}))).then_inc(s, 16)

            def load_lora_a(G):
                wait_alone(sp_e, sp_passed, full["xr"], G)
                load_adapters(G, 0, loraA, lambda b: GA[:, :, R * b:R * (b + 1)], ga_in)

            def load_lora_b(G):
                wait_alone(sp_e, sp_passed, full["cond"], K * G)
                load_adapters(G, 0, loraB, lambda b: GBA2[R * b:R * (b + 1), :], gb_in)

            def load_lora2(G):
                wait_alone(sp_e, sp_passed, full["A2T"], 2 * G)
                load_adapters(G, 1, lora2A, lambda b: GBA2[64 + R * b:64 + R * (b + 1), :], a2_in)
                wait_alone(sp_e, sp_passed, full["FB"], G)
                load_adapters(G, 1, lora2B, lambda b: B2g[:, :, R * b:R * (b + 1)], b2_in)

            def W_chunk(o):
                return Wst[:, o % 2, :, :, :].bitcast(fp32).rearrange("p h k o -> p (h k o)")

            def load_W(g, o):
                wait_alone(sp_e, sp_passed, full["cond"], K * g + o - 1)
                sp_e.dma_start(W_chunk(o), W_scratch[o]).then_inc(W_in[o % 2], 16)

            def put_stack(g, i):
                t, par = K * g + i, i % 2
                for hl, made in enumerate([hi_made, taken["dtxT"]]):
                    wait_alone(sp_e, sp_passed, made, t + 1, stack_in[par], 32 * (K // 2 * g + i // 2))
                    sp_e.dma_start(parts_scratch[par, hl].rearrange("p a t -> a p t"),
                                   parts[:, hl, :].bitcast(fp32)).then_inc(parts_out, 16)
                wait_alone(sp_e, sp_passed, parts_out, 32 * (t + 1), dBx_full, UNITS * (t - 1))
                for hl in range(2):
                    sp_e.dma_start(
                        stack[64 * hl:64 * (hl + 1), par, :, :, :].bitcast(fp32).rearrange("p a tt d -> p (a tt d)"),
                        parts_scratch[par, hl].rearrange("p a t -> p (a t)").unsqueeze(0).to_broadcast([2, QT, P // QT * T]))\
                        .then_inc(stack_in[par], 16)

            def load_xres(G, j, t):
                wait(sp_e, x1_made, t - 1)
                sp_e.dma_start(xres[:, j % 2, :, :], of_group(x_tok, G)[:, :, P * j:P * (j + 1)])\
                    .then_inc(xres_in[j % 2], 16)

            def put_c(G):
                wait(sp_e, bc_made, 3 * G + 3)
                dst = c_scratch[G] if isinstance(G, int) else c_scratch[DynSlice(G, 1)].rearrange("o a c -> (o a) c")
                for hh in range(2):
                    for p in range(2):
                        sp_e.dma_start(
                            dst[2 * hh + p].rearrange("(b n t) -> n b t", b=2, n=HS),
                            BC[48 + HS * hh:48 + HS * (hh + 1), p * P:(p + 1) * P].rearrange("n (b t) -> n b t", b=2))\
                            .then_inc(cscr_out, 16)

            def spread_c(G, un):
                if un == 0:
                    wait(sp_e, cscr_out, 64 * G + 64)
                wait(sp_e, hC_made, UNITS * K * G - UNITS + un + 1)
                src = c_scratch[G] if isinstance(G, int) else c_scratch[DynSlice(G, 1)].rearrange("o a c -> (o a) c")
                sp_e.dma_start(Cb[:, un, :], src[un:un + 1, :].to_broadcast([P, UNIT])).then_inc(C_in[un], 16)

            def store(G, i):
                wait_alone(sp_e, sp_passed, taken["out"], 4 * G + i + 1)
                tt, half = i // 2, i % 2
                sp_e.dma_start(of_group(out_tok, G)[:, tt, half * 512:(half + 1) * 512], obuf[:, i % 2, :])\
                    .then_inc(out_done[i % 2], 16)

            sp_e.dma_start(idx[0:1, 0, :], ids1.rearrange("(o n) -> o n", o=1)).then_inc(s_idx, 16)
            sp_e.dma_start(idx[0:1, 1, :], ids2.rearrange("(o n) -> o n", o=1)).then_inc(s_idx, 16)
            for i in range(4):
                load_x(sp_e, 0, i)
            sp_e.dma_start(xproj_n, xproj_w).then_inc(s_setw, 16)
            sp_e.dma_start(dtproj_n, dtproj_w.rearrange("(k p) r -> p k r", p=P)).then_inc(s_setw, 16)
            sp_e.dma_start(negA[:, :, :], A_log.rearrange("(k p) n -> p k n", p=P)).then_inc(s_par, 16)
            sp_e.dma_start(b_raw, dtproj_b.rearrange("(o n) -> o n", o=1)).then_inc(s_par, 16)
            for dst, src in ((Dsb, Dw), (bias_sb, bias2)):
                sp_e.dma_start(dst[:, :], src.rearrange("(k p) -> p k", p=P),
                               allow_slow_non_contiguous=True).then_inc(s_par, 16)
            sp_e.dma_start(F_n[0:EM, :], expA.rearrange("e r d -> (e r) d")).then_inc(s_F, 16)
            sp_e.dma_start(F_n[EM:EM + E, :], router_w).then_inc(s_F, 16)
            for e in range(E):
                sp_e.dma_start(expB_n[:, :, R * e:R * (e + 1)], expB[e].rearrange("(k p) r -> p k r", p=P))\
                    .then_inc(s_F, 16)
            for half in range(2):
                for a in range(2):
                    sp_e.dma_start(Wraw[a][:, :, half * 512:(half + 1) * 512],
                                   W.rearrange("(a k p) o -> a p k o", p=P, a=2)[a][:, :, half * 512:(half + 1) * 512])\
                        .then_inc((s_W0, s_W1)[half], 16)
                if half == 0:
                    sp_e.wait_ge(s_idx, 32)
                    load_lora_a(0)
                    load_lora_b(0)
            sp_e.wait_ge(b_split, 2)
            for i in range(2):
                sp_e.dma_start(dtprojT[3 * DTR + i:3 * DTR + i + 1, :].bitcast(fp32), b_part[i].bitcast(fp32)).then_inc(s_bias, 16)
            for o in range(K):
                sp_e.wait_ge(Wl_made, o + 1)
                sp_e.dma_start(W_scratch[o], W_chunk(o)).then_inc(W_out[o % 2], 16)
                if o >= 4:
                    sp_e.dma_start(W2c[o - 4], W2[P * (o - 4):P * (o - 3), :]).then_inc(s_W2[o - 4], 16)
            put_c(0)
            for k in range(4, K):
                wait(sp_e, gt_full, k - 3)
                sp_e.dma_start(W2c[k % 4], W2[P * k:P * (k + 1), :]).then_inc(s_W2[k % 4], 16)
            put_stack(0, 0)
            for un in range(UNITS):
                spread_c(0, un)
            for o in range(2):
                sp_e.wait_ge(W_out[o], 16 * K // 2)
                load_W(1, o)

            def body(G):
                last = isinstance(G, int) and G == GROUPS - 1
                first = isinstance(G, int) and G == 0
                for j in range(K):
                    t = K * G + j
                    for un in range(UNITS):
                        if un == 0:
                            if j:
                                load_xres(G, j - 1, t - 1)
                            elif not first:
                                load_xres(G - 1, K - 1, t - 1)
                        if (j, un) == (0, 0) and not last:
                            load_lora_a(G + 1)
                        if (j, un) == (0, 1):
                            if not first:
                                spread_c(G, UNITS - 1)
                            if not last:
                                load_lora_b(G + 1)
                        if (j, un) == (3, 2):
                            load_lora2(G)
                        for name, i, g in jobs_of(G, j, un):
                            if name == "dtxT":
                                put_stack(g, i)
                            if name == "Bst":
                                put_c(g)
                            if name == "cond" and i + 2 < K:
                                load_W(g, i + 2)
                            if name == "cond" and i + 2 >= K:
                                load_W(g + 1, i + 2 - K)
                            if name == "out":
                                store(g, i)
                        if j == K - 1 and un >= 1 and not last:
                            spread_c(G + 1, un - 1)

            groups(sp_e, body)
            load_xres(GROUPS - 1, K - 1, K * GROUPS - 1)
            for i in range(4):
                store(GROUPS - 1, i)
            for s in out_done:
                sp_e.wait_ge(s, 16 * 2 * GROUPS)
            sp_e.wait_ge(cscr_out, 64 * GROUPS)
            for s in W_in:
                sp_e.wait_ge(s, 16 * (K // 2 * (GROUPS - 1) + 1))

        @block.gpsimd
        def _(pool):
            made = 0

            def step(ins):
                nonlocal made
                made += 1
                ins.then_inc(s_cst, 1)
                pool.wait_ge(s_cst, made)

            def select(view, pattern, base, cm, op=ALU.not_equal, fill=1.0):
                step(pool.affine_select(out=view, in_=view, compare_op=op, fill=fill, base=base,
                                        pattern=pattern, channel_multiplier=cm))

            step(pool.memset(ident[:, :], 0.0))
            select(ident[:, :], [[-1, P]], 0, 1)
            step(pool.memset(own_batch[:, :], 1.0))
            v = own_batch[:, :].rearrange("p (b t) -> p b t", b=GB_)
            select(v, [[-R, GB_], [0, STEPS]], 0, 1, ALU.is_ge, 0.0)
            select(v, [[R, GB_], [0, STEPS]], R - 1, -1, ALU.is_ge, 0.0)
            step(pool.memset(own_rank[:, :, :], 0.0))
            for b in range(GB_):
                step(pool.memset(own_rank[STEPS * (b % 2):STEPS * (b % 2 + 1), b // 2, R * b:R * (b + 1)], 1.0))
            step(pool.memset(diag32[:, :], 0.0))
            for q in range(4):
                select(diag32[QT * q:QT * (q + 1), :], [[-1, QT]], 0, 1)
            step(pool.memset(before[:, :, :], 1.0))
            select(before[:, :, :], [[1, E], [-1, E]], 0, 0, ALU.is_gt, 0.0)
            for q in range(4):
                step(pool.memset(use_hi[QT * q:QT * (q + 1), :], float(q % 2 == 0)))
                step(pool.memset(use_lo[QT * q:QT * (q + 1), :], float(q % 2 == 1)))
            step(pool.memset(dtin[3 * DTR:, :].bitcast(fp32), 1.0))

            def make_dtx(t, i):
                pool.wait_ge(taken["dtz"], t + 1)
                wait(pool, full["dtxT"], t)
                pool.tensor_tensor(dtx[:, :], dt[:, i % NDT, :], u[:, i % K, :], ALU.mult).then_inc(dtx_made, 1)

            pool.wait_ge(taken["cond"], K)
            make_dtx(0, 0)
            make_dtx(1, 1)

            def body(G):
                for j in range(K):
                    for un in range(UNITS):
                        s = UNITS * (K * G + j) + un
                        pool.wait_ge(h_made, s + 1)
                        wait(pool, sum_done, s - NHC + 1)
                        if j == 0:
                            pool.wait_ge(C_in[un], 16 * G + 16)
                        pool.tensor_tensor(
                            hC[:, un % NHC, :].rearrange("p (n b t) -> p b n t", n=HS, b=2),
                            h[:, un % NH, :].rearrange("p (b n t) -> p b n t", n=HS, b=2),
                            Cb[:, un, :].rearrange("p (b n t) -> p b n t", n=HS, b=2), ALU.mult).then_inc(hC_made, 1)
                        for name, i, g in jobs_of(G, j, un - 1) if un else ():
                            if name == "dtz" and i != K:
                                make_dtx(K * g + i, i)
                        for name, i, g in jobs_of(G, j, un):
                            if (name, i) == ("dtz", K):
                                pool.wait_ge(taken["cond"], K * (g + 2))
                                make_dtx(K * g + i, i)

            groups(pool, body)

        @block.scalar
        def _(act):
            def softplus_parts(t, i, bank):
                act.wait_ge(full["dtz"], t + 1)
                wait(act, taken["dtz"], t)
                b = sp[:, :]
                act.activation(b, jb[bank][:, 0:T], ACT.Abs).then_inc(sp_step, 1)
                act.wait_ge(sp_step, 3 * t + 1)
                act.activation(b, b, ACT.Exp, scale=-1.0).then_inc(sp_step, 1)
                act.wait_ge(sp_step, 3 * t + 2)
                act.activation(b, b, ACT.Ln, bias=1.0).then_inc(sp_step, 1)
                wait(act, sum_done, UNITS * (t - 3))
                act.activation(Du[:, i % 4, :], u[:, i % K, :], ACT.Copy, scale=Dsb[:, i % K:i % K + 1]).then_inc(Du_made, 1)

            def decays(G, j, half, part):
                q = 2 * (K * G + j) + half
                if part == 0:
                    act.wait_ge(taken["dtz"], K * G + j + 1)
                    wait(act, h_made, 2 * (q - NDA) + 2)
                for n in range(4 * part, 4 * part + 4):
                    act.activation(
                        dA[:, half % NDA, :].rearrange("p (b n t) -> p b n t", b=GB_, n=HS)[:, :, n, 1:STEPS],
                        dt[:, j % NDT, :].rearrange("p (b t) -> p b t", b=GB_)[:, :, 1:STEPS],
                        ACT.Exp, scale=negA[:, j, HS * half + n:HS * half + n + 1]).then_inc(dA_made, 1)

            def job(name, i, g, bank):
                psum = None if bank is None else jb[bank]
                if name == "dtz":
                    return softplus_parts(K * g + i, i, bank)
                if name in ("xr", "mid", "gate", "out"):
                    return
                if name == "GAs":
                    act.wait_ge(ga_in, 64 * g + 64)
                    wait(act, full["xr"], g)
                    act.activation(GAs[:, 0, :, :], GA[:, :, :], ACT.Copy).then_inc(GAh_made, 1)
                    return
                if name == "mid2":
                    act.wait_ge(gate_step, GATE_STEPS * g + 2)
                    act.activation(gate[:, 1, :], gate[:, 0, :], ACT.Exp).then_inc(gate_exp, 1)
                    return
                act.wait_ge(full[name], nth(name, g, i))
                if name == "dtxT":
                    t = K * g + i
                    wait(act, parts_out, 32 * t)
                    act.activation(parts[:, 0, :], psum[:, 0:T], ACT.Copy).then_inc(hi_made, 1)
                elif name == "x1T":
                    act.activation(x1T[:, i % K, :], psum[:, 0:T], ACT.Copy).then_inc(taken[name], 1)
                elif name == "xT":
                    act.activation(xT[:, 0, 2 * i:2 * i + 2, :].rearrange("p k t -> p (k t)"), psum[:, :], ACT.Copy)\
                        .then_inc(xh_made, 1)
                elif name == "cond":
                    wait(act, dtx_made, K * (g - 1) + i + 1)
                    wait(act, Du_made, K * (g - 1) + i + 1)
                    act.activation(u[:, i, :], psum[:, 0:T], ACT.Copy).then_inc(taken[name], 1)
                elif name == "xproj":
                    wait(act, cscr_out, 64 * g)
                    for s in out_done:
                        wait(act, s, 32 * (g - 1))
                    act.activation(dtin[0:DTR, :], psum[0:DTR, 0:T], ACT.Copy).then_inc(dtin_hi, 1)
                    act.wait_ge(dtin_hi, g + 1)
                    act.activation(dtin[DTR:2 * DTR, :], dtin[0:DTR, :].bitcast(fp32), ACT.Copy).then_inc(bc_made, 1)
                    act.activation(BC[DTR:2 * DTR, :], psum[DTR:2 * DTR, 0:T], ACT.Copy).then_inc(bc_made, 1)
                    act.activation(
                        B4[DTR:2 * DTR, :].rearrange("p (q a t) -> p q a t", q=NQ, a=4),
                        psum[DTR:2 * DTR, 0:T].rearrange("p (q t) -> p q t", q=NQ).unsqueeze(2)
                        .to_broadcast([DTR, NQ, 4, QT]), ACT.Copy).then_inc(bc_made, 1)
                elif name == "Bst":
                    act.activation(Bhl[:, 0, :], psum[:, 0:NQ * R], ACT.Copy).then_inc(b_step, 1)
                elif name == "A2T":
                    act.activation(G2[:, 4 * i:4 * i + 4, EM + E:], psum[:, 0:256].rearrange("p (k m) -> p k m", k=4),
                                   ACT.Copy).then_inc(taken[name], 1)
                elif name == "FB":
                    act.activation(FB[64:P, :], psum[64:P, 0:EM + E], ACT.Copy).then_inc(taken[name], 1)
                elif name == "h2T":
                    act.activation(low[64:P, :], psum[0:64, 0:T], ACT.Copy).then_inc(taken[name], 1)
                elif name == "gm":
                    act.activation(gm[:, :], psum[0:EM, 0:T], ACT.Copy).then_inc(taken[name], 1)

            act.add_instruction(mybir.InstLoadActFuncSet(name=nc.get_next_instruction_name(), act_func_set_id=LN_EXP_TABLES))
            act.wait_ge(s_par, 64)
            act.activation(b_part[0], b_raw, ACT.Copy).then_inc(b_split, 1)
            act.activation(negA[:, :, :], negA[:, :, :], ACT.Exp).then_inc(s_neg, 1)
            act.wait_ge(s_neg, 1)
            act.mul(negA[:, :, :], negA[:, :, :], -1.0).then_inc(s_neg, 1)
            act.wait_ge(s_neg, 2)
            act.wait_ge(set_full, 1)
            act.activation(xprojT[:, :, :].rearrange("p k m -> p (k m)"), jb[0][:, :], ACT.Copy).then_inc(set_taken, 1)
            for i in range(2):
                act.wait_ge(set_full, 2 + i)
                c = slice(512 * i, 512 * (i + 1))
                act.activation(dtprojT[0:DTR, c], jb[1 - i][0:DTR, :], ACT.Copy).then_inc(w_hi, 1)
                act.wait_ge(w_hi, 2 * i + 1)
                act.activation(dtprojT[2 * DTR:3 * DTR, c], dtprojT[0:DTR, c].bitcast(fp32), ACT.Copy).then_inc(w_hi, 1)
            for i in range(4):
                job("xT", i, 0, (i + 1) % 2)
            for i in range(2):
                act.wait_ge(set_full, 4 + i)
                act.activation(FT[:, 4 * i:4 * i + 4, :].rearrange("p k m -> p (k m)"), jb[1 - i][:, 0:4 * (EM + E)], ACT.Copy)\
                    .then_inc(set_taken, 1)
            for i in range(2):
                act.wait_ge(set_full, 6 + i)
                act.activation(expBT[:, 512 * i:512 * (i + 1)], jb[1 - i][0:EM, :], ACT.Copy).then_inc(set_taken, 1)
            def W_high(o):
                if o < 2:
                    act.wait_ge((s_W0, s_W1)[o // 4], 32)
                else:
                    act.wait_ge(full["cond"], o - 1)
                    act.wait_ge(W_out[o % 2], 16 * (o // 2))
                    act.wait_ge((s_W0, s_W1)[o // 4], 32)
                for a in range(2):
                    last = act.activation(Wst[:, o % 2, 0, K // 2 * a:K // 2 * (a + 1), :], Wraw[a][:, :, P * o:P * (o + 1)], ACT.Copy)
                last.then_inc(Wh_made, 1)

            job("GAs", 0, 0, None)
            W_high(0)
            W_high(1)
            for o in range(K):
                job("cond", o, 0, o % 2)
                if o + 2 < K:
                    W_high(o + 2)
            job("xproj", 0, 0, 0)
            job("dtz", 0, 0, 1)
            job("Bst", 0, 0, 0)
            job("dtz", 1, 0, 1)
            job("dtxT", 0, 0, 0)
            act.wait_ge(s_cstv, 1)
            decays(0, 0, 0, 0)
            decays(0, 0, 0, 1)
            act.wait_ge(gt_full, K)
            for i in range(2):
                act.activation(G_n[:, 512 * i:512 * (i + 1)], yp[i][0:EM + E, :], ACT.Copy).then_inc(gt_taken, 1)
            for i in range(2):
                act.wait_ge(set_full, 8 + i)
                act.activation(G2[:, 4 * i:4 * i + 4, 0:EM + E], jb[i][:, 0:4 * (EM + E)].rearrange("p (k m) -> p k m", k=4),
                               ACT.Copy).then_inc(set_taken, 1)
            act.wait_ge(set_full, 10)
            act.activation(cF[:, :], jb[0][:, 0:EM + E], ACT.Copy).then_inc(set_taken, 1)

            def body(G):
                last = isinstance(G, int) and G == GROUPS - 1
                if not last:
                    for i in range(4):
                        load_x(act, G + 1, i)
                for j in range(K):
                    for un in range(UNITS):
                        nj, nhalf = (j, 1) if un < 2 else (j + 1, 0)
                        if not (last and nj == K) and un in DECAYS_FIRST:
                            decays(G if nj < K else G + 1, nj % K, nhalf, un % 2)
                        for name, i, g in jobs_of(G, j, un):
                            job(name, i, g, BANK[name, i])
                        if not (last and nj == K) and un not in DECAYS_FIRST:
                            decays(G if nj < K else G + 1, nj % K, nhalf, un % 2)

            groups(act, body)
            job("x1T", K - 2, GROUPS - 1, 0)
            job("x1T", K - 1, GROUPS - 1, 1)
            job("h2T", 0, GROUPS - 1, 1)
            job("mid2", 0, GROUPS - 1, 0)
            job("gm", 0, GROUPS - 1, 1)

        @block.vector
        def _(dve):
            def step_size(t, i, bank):
                dve.wait_ge(sp_step, 3 * t + 3)
                wait(dve, dA_made, R * (t - NDT + 1))
                dve.scalar_tensor_tensor(dt[:, i % NDT, :], jb[bank][:, 0:T], 0.0, sp[:, :], ALU.max, ALU.add)\
                    .then_inc(taken["dtz"], 1)

            def add_residual(G, j, t):
                dve.wait_ge(sum_done, UNITS * (t + 1))
                dve.wait_ge(xres_in[j % 2], 16 * (K // 2 * G + j // 2 + 1))
                if j == 0:
                    wait(dve, taken["out"], 4 * G)
                dve.tensor_tensor(x1[:, :, P * j:P * (j + 1)], yp[j % 2][:, 0:T].rearrange("p (tt d) -> p tt d", tt=TT),
                                  xres[:, j % 2, :, :], ALU.add).then_inc(x1_made, 1)

            def b_diagonals(G, un):
                dve.wait_ge(b_step, 4 * G + 4)
                half, p = un // 2, un % 2
                of = [P, NQ // 2, HS, QT]
                dve.tensor_tensor(
                    Bd[:, NQ // 2 * p:NQ // 2 * (p + 1), HS * half:HS * (half + 1), :],
                    Bst[:, :].bitcast(fp32).rearrange("p (q n) -> p q n", q=NQ)
                    [:, NQ // 2 * p:NQ // 2 * (p + 1), HS * half:HS * (half + 1)].unsqueeze(3).to_broadcast(of),
                    diag32[:, :].unsqueeze(1).unsqueeze(1).to_broadcast(of), ALU.mult).then_inc(Bd_made, 1)

            def te(i):
                return gate[:, i, :].rearrange("p (a e) -> p a e", a=TT)

            def ee(i):
                return beats[:, i, :].rearrange("p (a e f) -> p (a e) f", e=E, f=E)

            def gating(g, second):
                n = 6 if second else 0

                def link(ins):
                    nonlocal n
                    n += 1
                    ins.then_inc(gate_step, 1)
                    dve.wait_ge(gate_step, GATE_STEPS * g + n)

                shape = [P, TT, E]
                if not second:
                    logits = mids[:, :, EM:EM + E]
                    top = gate[:, 2, 0:TT]
                    link(dve.tensor_reduce(top, logits, AX.X, ALU.max))
                    link(dve.tensor_tensor(te(0), logits, top.unsqueeze(2).to_broadcast(shape), ALU.subtract))
                    for tt in range(TT):
                        other = logits[:, tt, :].unsqueeze(1).to_broadcast([P, E, E])
                        own = logits[:, tt, :].unsqueeze(2).to_broadcast([P, E, E])
                        dve.tensor_tensor(ee(0)[:, E * tt:E * (tt + 1), :], other, own, ALU.is_gt)
                        last = dve.tensor_tensor(ee(1)[:, E * tt:E * (tt + 1), :], other, own, ALU.is_equal)
                    link(last)
                    for tt in range(TT):
                        last = dve.tensor_tensor(ee(1)[:, E * tt:E * (tt + 1), :], ee(1)[:, E * tt:E * (tt + 1), :],
                                                 before[:, :, :], ALU.mult)
                    link(last)
                    link(dve.tensor_tensor(beats[:, 0, :], beats[:, 0, :], beats[:, 1, :], ALU.add))
                    link(dve.tensor_reduce(gate[:, 3, :], ee(0), AX.X, ALU.add))
                    assert n == 6
                    return
                dve.wait_ge(gate_exp, g + 1)
                link(dve.scalar_tensor_tensor(gate[:, 1, :], gate[:, 3, :], 1.5, gate[:, 1, :], ALU.is_lt, ALU.mult))
                link(dve.tensor_reduce(gate[:, 2, 0:TT], te(1), AX.X, ALU.add))
                link(dve.reciprocal(gate[:, 3, 0:TT], gate[:, 2, 0:TT]))
                link(dve.scalar_tensor_tensor(te(4), te(1), LORA2_SCALE, gate[:, 3, 0:TT].unsqueeze(2).to_broadcast(shape),
                                              ALU.mult, ALU.mult))
                assert n == GATE_STEPS
                for tt in range(TT):
                    last = dve.tensor_tensor(
                        gmT[:, tt, :].rearrange("p (e r) -> p e r", e=E),
                        mids[:, tt, 0:EM].rearrange("p (e r) -> p e r", e=E),
                        te(4)[:, tt, :].unsqueeze(2).to_broadcast([P, E, R]), ALU.mult)
                last.then_inc(gated, 1)

            def job(name, i, g, bank):
                if name == "gate":
                    return gating(g, True)
                if name == "GAs":
                    dve.wait_ge(GAh_made, g + 1)
                    dve.tensor_tensor(GAs[:, 1, :, :], GA[:, :, :], GAs[:, 0, :, :].bitcast(fp32), ALU.subtract).then_inc(GA_split, 1)
                    return
                psum = jb[bank]
                if name == "dtz":
                    return step_size(K * g + i, i, bank)
                if name == "dtxT":
                    t = K * g + i
                    dve.wait_ge(hi_made, t + 1)
                    dve.tensor_tensor(parts[:, 1, :], psum[:, 0:T], parts[:, 0, :].bitcast(fp32), ALU.subtract)\
                        .then_inc(taken[name], 1)
                elif name == "xT":
                    dve.wait_ge(xh_made, 4 * g + i + 1)
                    dve.tensor_tensor(xT[:, 1, 2 * i:2 * i + 2, :].rearrange("p k t -> p (k t)"), psum[:, :],
                                      xT[:, 0, 2 * i:2 * i + 2, :].rearrange("p k t -> p (k t)").bitcast(fp32), ALU.subtract)\
                        .then_inc(taken[name], 1)
                elif name == "xr":
                    dve.wait_ge(full[name], g + 1)
                    dve.tensor_tensor(low[0:64, :], psum[0:64, 0:T], own_batch[0:64, :], ALU.mult).then_inc(taken[name], 1)
                elif name == "xproj":
                    dve.wait_ge(dtin_hi, g + 1)
                    dve.tensor_tensor(dtin[2 * DTR:3 * DTR, :], psum[0:DTR, 0:T], dtin[0:DTR, :].bitcast(fp32), ALU.subtract)\
                        .then_inc(dtin_lo, 1)
                elif name == "Bst":
                    dve.wait_ge(b_step, 4 * g + 1)
                    dve.tensor_tensor(Bhl[:, 1, :], psum[:, 0:NQ * R], Bhl[:, 0, :].bitcast(fp32), ALU.subtract)\
                        .then_inc(b_step, 1)
                    dve.wait_ge(b_step, 4 * g + 2)
                    dve.tensor_scalar(Bst[:, :], Bhl[:, 0, :].bitcast(fp32), use_hi[:, :], None, ALU.mult).then_inc(b_step, 1)
                    dve.wait_ge(b_step, 4 * g + 3)
                    dve.scalar_tensor_tensor(Bst[:, :], Bhl[:, 1, :].bitcast(fp32), use_lo[:, :], Bst[:, :].bitcast(fp32),
                                             ALU.mult, ALU.add).then_inc(b_step, 1)
                elif name == "mid":
                    dve.wait_ge(h2_raw, g + 1)
                    dve.tensor_tensor(h2m[:, :, :], psum[:, 0:TT * G2W].rearrange("p (a c) -> p a c", a=TT)[:, :, EM + E:],
                                      own_rank[:, :, :], ALU.mult).then_inc(h2_masked, 1)
                elif name == "mid2":
                    dve.wait_ge(full["mid"], g + 1)
                    dve.tensor_tensor(mids[:, :, :], psum[:, 0:TT * G2W].rearrange("p (a c) -> p a c", a=TT)[:, :, 0:EM + E],
                                      cF[:, :].unsqueeze(1).to_broadcast([P, TT, EM + E]), ALU.add).then_inc(taken["mid"], 1)
                    dve.wait_ge(taken["mid"], g + 1)
                    gating(g, False)
                elif name == "out":
                    dve.wait_ge(full[name], 4 * g + i + 1)
                    if i >= 2:
                        wait(dve, out_done[i % 2], 16 * (2 * g + 1))
                    tt, half = i // 2, i % 2
                    dve.tensor_tensor(obuf[:, i % 2, :], psum[:, :], x1[:, tt, half * 512:(half + 1) * 512], ALU.add)\
                        .then_inc(taken[name], 1)

            dve.wait_ge(s_cst, CONSTS)
            dve.wait_ge(b_split, 1)
            dve.tensor_tensor(b_part[1], b_raw, b_part[0].bitcast(fp32), ALU.subtract).then_inc(b_split, 1)
            for i in range(2):
                c = slice(512 * i, 512 * (i + 1))
                dve.wait_ge(w_hi, 2 * i + 1)
                dve.tensor_tensor(dtprojT[DTR:2 * DTR, c], jb[1 - i][0:DTR, :], dtprojT[0:DTR, c].bitcast(fp32), ALU.subtract)\
                    .then_inc(set_taken, 1)
            for i in range(4):
                job("xT", i, 0, (i + 1) % 2)
            job("GAs", 0, 0, None)
            for o in range(K):
                dve.wait_ge(Wh_made, o + 1)
                for a in range(2):
                    last = dve.tensor_tensor(Wst[:, o % 2, 1, K // 2 * a:K // 2 * (a + 1), :], Wraw[a][:, :, P * o:P * (o + 1)],
                                             Wst[:, o % 2, 0, K // 2 * a:K // 2 * (a + 1), :].bitcast(fp32), ALU.subtract)
                last.then_inc(Wl_made, 1)
                if o == 0:
                    job("xr", 0, 0, 1)
            dve.wait_ge(Wl_made, K)
            for i in range(NDA):
                last = dve.memset(dA[:, i, :].rearrange("p (b n t) -> p (b n) t", b=GB_, n=HS)[:, :, 0:1], 0.0)
            last.then_inc(s_cstv, 1)
            job("xproj", 0, 0, 0)
            job("dtz", 0, 0, 1)
            job("Bst", 0, 0, 0)
            for un in range(UNITS):
                b_diagonals(0, un)
            job("dtz", 1, 0, 1)
            job("dtxT", 0, 0, 0)

            def body(G):
                first, final = (isinstance(G, int) and G == g for g in (0, GROUPS - 1))
                for j in range(K):
                    t = K * G + j
                    for un in range(UNITS):
                        s, half, p = UNITS * t + un, un // 2, un % 2
                        if un == UNITS - 1 and j == 0 and not first:
                            add_residual(G - 1, K - 1, t - 1)
                        if un == UNITS - 1 and j == 2:
                            add_residual(G, 0, t - 2)
                        if un == UNITS - 1 and j >= 2:
                            add_residual(G, j - 1, t - 1)
                        dve.wait_ge(dBx_full, s + 1)
                        dve.wait_ge(dA_made, R * t + HS * (half + 1))
                        wait(dve, hC_made, s - NH + 1)
                        dve.tensor_tensor_scan(h[:, un % NH, :], dA[:, half % NDA, UNIT * p:UNIT * (p + 1)], dBx[un % 2][:, :],
                                               0.0, ALU.mult, ALU.add).then_inc(h_made, 1)
                        if j == K - 1 and not final:
                            b_diagonals(G + 1, un)
                        for name, i, g in jobs_of(G, j, un - 1) if un else ():
                            if (name, i) in LATE:
                                job(name, i, g, BANK[name, i])
                        for name, i, g in jobs_of(G, j, un):
                            if (name, i) not in LATE:
                                job(name, i, g, BANK[name, i])

            groups(dve, body)
            add_residual(GROUPS - 1, K - 1, K * GROUPS - 1)
            job("mid", 0, GROUPS - 1, 0)
            job("mid2", 0, GROUPS - 1, 0)
            job("gate", 0, GROUPS - 1, 0)
            for i in range(4):
                job("out", i, GROUPS - 1, i % 2)

        @block.tensor
        def _(pe):
            tenant = {}

            def mm(o, lhsT, rhs, start, stop, **kw):
                return pe.matmul(o, lhsT, rhs, start=start, stop=stop, **kw)

            def tr(o, in_, n, first=0):
                return pe.matmul(o, in_, ident[first:first + n, first:first + n], is_transpose=True, start=True, stop=True)

            def job(name, i, g, bank):
                operand = {"Bst": (bc_made, 3 * g + 3), "A2T": (a2_in, 64 * g + 64),
                           "h2T": (h2_masked, g + 1), "gm": (gated, g + 1)}.get(name, ())
                if name in ("gate", "GAs"):
                    return
                if name == "mid2":
                    psum = jb[bank]
                    pe.wait_ge(taken["h2T"], g + 1)
                    pe.wait_ge(taken["FB"], g + 1)
                    for tt in range(TT):
                        last = mm(psum[:, G2W * tt:G2W * tt + EM + E], low[64:P, P * tt:P * (tt + 1)], FB[64:P, :],
                                  False, True, skip_group_check=True)
                    last.then_inc(full["mid"], 1)
                    return
                if operand:
                    wait_alone(pe, pe_passed, *tenant.get(bank, ()), *operand)
                elif bank in tenant:
                    for s, v in zip(tenant[bank][::2], tenant[bank][1::2]):
                        wait(pe, s, v)
                tenant[bank] = (taken[name], nth(name, g, i))
                psum = jb[bank]
                if name == "dtz":
                    pe.wait_ge(bc_made, 3 * (g if i < K else g + 1) + 1)
                    pe.wait_ge(dtin_lo, (g if i < K else g + 1) + 1)
                    last = mm(psum[:, 0:T], dtprojT[:, P * (i % K):P * (i % K + 1)], dtin[:, :], True, True)
                elif name == "dtxT":
                    pe.wait_ge(dtx_made, K * g + i + 1)
                    for tt in range(TT):
                        last = tr(psum[:, P * tt:P * (tt + 1)], dtx[:, P * tt:P * (tt + 1)], P)
                elif name == "x1T":
                    pe.wait_ge(x1_made, K * g + i + 1)
                    for tt in range(TT):
                        last = tr(psum[:, P * tt:P * (tt + 1)], x1[:, tt, P * (i % K):P * (i % K + 1)], P)
                elif name == "xT":
                    pe.wait_ge(xin_in[i], 16 * (g + 1))
                    for a in range(2):
                        for tt in range(TT):
                            c = (a * TT + tt) * P
                            last = tr(psum[:, c:c + P], xin[:, i, tt, P * a:P * (a + 1)], P)
                elif name == "xr":
                    pe.wait_ge(taken["xT"], 4 * g + 4)
                    pe.wait_ge(GA_split, g + 1)
                    for k in range(K):
                        for n, (a, b) in enumerate(PARTS):
                            last = mm(psum[0:64, 0:T], GAs[:, a, k, :], xT[:, b, k, :], k == 0 and n == 0, k == K - 1 and n == 2)
                elif name == "cond":
                    if isinstance(g, int) and g == 0:
                        pe.wait_ge(Wl_made, i + 1)
                    else:
                        pe.wait_ge(W_in[i % 2], 16 * (K // 2 * (g - 1) + i // 2 + 1))
                    for k in range(K):
                        for n, (a, b) in enumerate(PARTS):
                            mm(psum[:, 0:T], Wst[:, i % 2, a, k, :], xT[:, b, k, :], k == 0 and n == 0, False)
                    if i == 0:
                        pe.wait_ge(taken["xr"], g + 1)
                        pe.wait_ge(gb_in, 64 * g + 64)
                    last = mm(psum[:, 0:T], GBA2[0:64, P * i:P * (i + 1)], low[0:64, :], False, True)
                elif name == "xproj":
                    pe.wait_ge(taken["cond"], K * g + K)
                    for k in range(K):
                        last = mm(psum[0:2 * DTR, 0:T], xprojT[:, k, :], u[:, k, :], k == 0, k == K - 1)
                    tenant[bank] = (bc_made, 3 * g + 3, dtin_lo, g + 1)
                elif name == "Bst":
                    for q in range(NQ):
                        last = pe.matmul(psum[:, R * q:R * (q + 1)], B4[DTR:DTR + R, P * q:P * (q + 1)],
                                         ident[DTR:DTR + R, DTR:DTR + R], is_transpose=True, start=True, stop=True)
                    tenant[bank] = (b_step, 4 * g + 2)
                elif name == "A2T":
                    for a in range(4):
                        k = 4 * i + a
                        last = tr(psum[:, 64 * a:64 * (a + 1)], GBA2[64:P, P * k:P * (k + 1)], 64, 64)
                elif name == "FB":
                    pe.wait_ge(b2_in, 64 * g + 64)
                    for k in range(K):
                        last = mm(psum[64:P, 0:EM + E], B2g[:, k, :], FT[:, k, :], k == 0, k == K - 1)
                elif name == "mid":
                    pe.wait_ge(taken["x1T"], K * g + K)
                    pe.wait_ge(taken["A2T"], 2 * g + 2)
                    for tt in range(TT):
                        for k in range(K):
                            last = mm(psum[:, G2W * tt:G2W * (tt + 1)], x1T[:, k, P * tt:P * (tt + 1)], G2[:, k, :],
                                      k == 0 and tt == 0, False, skip_group_check=True)
                    last.then_inc(h2_raw, 1)
                    return
                elif name == "h2T":
                    for tt in range(TT):
                        last = tr(psum[0:64, P * tt:P * (tt + 1)], h2m[:, tt, :], P)
                elif name == "gm":
                    for tt in range(TT):
                        last = tr(psum[0:EM, P * tt:P * (tt + 1)], gmT[:, tt, :], P)
                elif name == "out":
                    pe.wait_ge(taken["gm"], g + 1)
                    tt, half = i // 2, i % 2
                    last = mm(psum[:, :], gm[:, P * tt:P * (tt + 1)], expBT[:, half * 512:(half + 1) * 512], True, True)
                last.then_inc(full[name], 1)

            def b_times_dtx(G, j, un):
                t = K * G + j
                s, half, p = UNITS * t + un, un // 2, un % 2
                if un == 0:
                    pe.wait_ge(stack_in[j % 2], 32 * (K // 2 * G + j // 2 + 1))
                if j == 0:
                    pe.wait_ge(Bd_made, UNITS * G + un + 1)
                wait(pe, h_made, s - 1)
                for b in range(2):
                    for a in range(2):
                        q = 4 * p + 2 * b + a
                        o = dBx[un % 2][:, 512 * b:512 * (b + 1)].rearrange("p (n t) -> p n t", n=HS)[:, :, QT * a:QT * (a + 1)]
                        last = mm(o, stack[:, j % 2, q % 4, q // 4, :],
                                  Bd[:, q, HS * half:HS * (half + 1), :].rearrange("p n t -> p (n t)"),
                                  True, True, skip_group_check=True)
                last.then_inc(dBx_full, 1)

            def sum_states(G, j, un):
                t = K * G + j
                half, p = un // 2, un % 2
                pe.wait_ge(hC_made, UNITS * t + un + 1)
                if un == 0:
                    wait(pe, x1_made, t - 1)
                y = yp[j % 2][:, P * p:P * (p + 1)]
                for n in range(HS):
                    last = pe.matmul(y, hC[:, un % NHC, P * n:P * (n + 1)], ident[:, :], is_transpose=True,
                                     start=un == 0 and n == 0, stop=False, skip_group_check=True)
                if half == 1:
                    if p == 0:
                        pe.wait_ge(Du_made, t + 1)
                    last = pe.matmul(y, Du[:, j % 4, P * p:P * (p + 1)], ident[:, :], is_transpose=True,
                                     start=False, stop=True, skip_group_check=True)
                last.then_inc(sum_done, 1)

            def set_up(bank, n):
                wait(pe, set_taken, n)

            pe.wait_ge(s_cst, CONSTS)
            pe.wait_ge(s_setw, 32)
            for k in range(K):
                last = tr(jb[0][:, 64 * k:64 * (k + 1)], xproj_n[:, P * k:P * (k + 1)], 64)
            last.then_inc(set_full, 1)
            for i in range(2):
                set_up(1 - i, i)
                for a in range(4):
                    last = tr(jb[1 - i][0:DTR, P * a:P * (a + 1)], dtproj_n[:, 4 * i + a, :], P)
                last.then_inc(set_full, 1)
            tenant[1], tenant[0] = (set_taken, 2), (set_taken, 3)
            for i in range(4):
                job("xT", i, 0, (i + 1) % 2)
            pe.wait_ge(s_F, 96)
            n = EM + E
            for i in range(2):
                wait(pe, taken["xT"], 3 + i)
                for a in range(4):
                    last = tr(jb[1 - i][:, n * a:n * (a + 1)], F_n[:, P * (4 * i + a):P * (4 * i + a + 1)], n)
                last.then_inc(set_full, 1)
            for i in range(2):
                set_up(1 - i, 4 + i)
                for a in range(4):
                    last = tr(jb[1 - i][0:EM, P * a:P * (a + 1)], expB_n[:, 4 * i + a, :], P)
                last.then_inc(set_full, 1)
            tenant[1], tenant[0] = (set_taken, 6), (set_taken, 7)
            job("xr", 0, 0, 1)
            for o in range(K):
                job("cond", o, 0, o % 2)
            pe.wait_ge(s_par, 64)
            pe.wait_ge(s_bias, 32)
            job("xproj", 0, 0, 0)

            def times_W2(k):
                pe.wait_ge(s_W2[k % 4], 16 * (k // 4 + 1))
                for c in range(2):
                    last = mm(yp[c][0:n, :], FT[:, k, :], W2c[k % 4][:, 512 * c:512 * (c + 1)], k == 0, k == K - 1)
                last.then_inc(gt_full, 1)

            times_W2(0)
            job("dtz", 0, 0, 1)
            times_W2(1)
            job("Bst", 0, 0, 0)
            times_W2(2)
            job("dtz", 1, 0, 1)
            times_W2(3)
            job("dtxT", 0, 0, 0)
            for k in range(4, K):
                times_W2(k)
            wait_alone(pe, pe_passed, gt_taken, 2, taken["dtz"], 2, taken["dtxT"], 1)
            for i in range(2):
                for a in range(4):
                    last = tr(jb[i][:, n * a:n * (a + 1)], G_n[:, P * (4 * i + a):P * (4 * i + a + 1)], n)
                last.then_inc(set_full, 1)
            wait(pe, set_taken, 8)
            for k in range(K):
                last = mm(jb[0][:, 0:n], bias_sb[:, k:k + 1].to_broadcast([P, P]), FT[:, k, :], k == 0, k == K - 1)
            last.then_inc(set_full, 1)
            pe.wait_ge(set_taken, 10)

            def body(G):
                first = isinstance(G, int) and G == 0
                tenant.clear()
                if not first:
                    for bank, (name, i) in LAST_JOB.items():
                        tenant[bank] = (taken[name], nth(name, G - 1, i))
                for j in range(K):
                    for un in range(UNITS):
                        b_times_dtx(G, j, un)
                        back = UNITS * j + un - LAG
                        if back >= 0:
                            sum_states(G, back // UNITS, back % UNITS)
                        elif not first:
                            sum_states(G - 1, K - 1, back % UNITS)
                        for name, i, g in jobs_of(G, j, un):
                            job(name, i, g, BANK[name, i])

            groups(pe, body)
            G = GROUPS - 1
            for un in range(UNITS - LAG, UNITS):
                sum_states(G, K - 1, un)
            job("x1T", K - 2, G, 0)
            job("x1T", K - 1, G, 1)
            job("mid", 0, G, 0)
            job("h2T", 0, G, 1)
            job("mid2", 0, G, 0)
            job("gm", 0, G, 1)
            for i in range(4):
                job("out", i, G, i % 2)


LN_EXP_TABLES = 6
GATE_STEPS = 10
DECAYS_FIRST = (1, 2, 3)
G2W = EM + E + GB_ * R
CONSTS = 26

_INS = ['x', 'itok_B_0_15', 'itok_B_6_15', 'L0_cond_W', 'L0_cond_lora_A', 'L0_cond_lora_B', 'L0_attn_A_log', 'L0_attn_D',
        'L0_attn_x_proj_w', 'L0_attn_dt_proj_w', 'L0_attn_dt_proj_b', 'L0_cond2_base_weight', 'L0_cond2_base_bias',
        'L0_cond2_lora_A_w', 'L0_cond2_lora_B_w', 'L0_ffn_router_w', 'L0_ffn_A', 'L0_ffn_B']


def kernel(**inputs):
    import numpy as _np
    import concourse.bacc as _bacc
    from concourse import mybir as _mybir
    from concourse.bass_utils import run_bass_kernel_spmd as _run

    nc = _bacc.Bacc("TRN2", target_bir_lowering=False, num_devices=1)
    arrays, args = {}, []
    for name in _INS:
        a = _np.ascontiguousarray(inputs[name])
        arrays[f"in_{name}"] = a
        args.append(nc.dram_tensor(f"in_{name}", a.shape, _mybir.dt.from_np(a.dtype), kind="ExternalInput").ap())
    o = nc.dram_tensor("out_0", (BATCHES, STEPS, D), _mybir.dt.float32, kind="ExternalOutput").ap()
    layer_kernel(nc, *args, o)
    r = _run(nc, [arrays], core_ids=[0])
    return r.results[0]["out_0"]
```
